# Optimizing a Trainium2 kernel written in Bass

```python
import numpy as np
import jax
import jax.numpy as jnp

def _softmax(x, axis=-1):
    return jax.nn.softmax(x, axis=axis)

def _gelu(x):
    return jax.nn.gelu(x, approximate=True)

def _silu(x):
    return jax.nn.silu(x)

def _sigmoid(x):
    return jax.nn.sigmoid(x)

def _layernorm(x, axis=-1, eps=1e-05):
    m = jnp.mean(x, axis=axis, keepdims=True)
    v = jnp.var(x, axis=axis, keepdims=True)
    return (x - m) / jnp.sqrt(v + eps)

def _scatter_add(tgt, idx, src, axis=0):
    return tgt.at[idx].add(src)

def _segment_sum(src, seg, n):
    return jax.ops.segment_sum(src, seg, n)
kernel_name = 'mk_xattn_seq_d4_seqx_r2_4af5ff'

def setup_inputs(seed: int=0):
    np.random.seed(seed)
    _w = jnp.asarray

    def _rec_inputs():
        import jax
        import jax.numpy as jnp
        _rk = jax.random.key(seed)
        x = -0.000125 + 0.9999 * jax.random.normal(jax.random.fold_in(_rk, 1), (2, 2048, 512), jnp.float32)
        _lenS = 2048 - jax.random.randint(jax.random.fold_in(_rk, 7), (2,), 0, max(1, 2048 // 4) + 1, jnp.int32)
        _lenS2 = 77 - jax.random.randint(jax.random.fold_in(_rk, 8), (2,), 0, max(1, 77 // 4) + 1, jnp.int32)
        _ctx_2048P = jax.random.normal(jax.random.fold_in(_rk, 11), (2, 16, 1024), jnp.float32)
        _ctx_2048c = jax.random.dirichlet(jax.random.fold_in(_rk, 511), 0.3 * jnp.ones((16,), jnp.float32), (2, 77))
        _ctx_2048t = jnp.einsum('bsk,bkd->bsd', _ctx_2048c, _ctx_2048P)
        _ctx_2048t = _ctx_2048t * jax.lax.rsqrt(jnp.mean(jnp.square(_ctx_2048t)) + 1e-12) * 0.953939
        ctx_2048 = 5.36139e-06 + 1.00015 * (_ctx_2048t + 0.3 * jax.random.normal(jax.random.fold_in(_rk, 611), (2, 77, 1024), jnp.float32))
        _validS = jnp.arange(2048)[None, :] < _lenS[:, None]
        _validS2 = jnp.arange(77)[None, :] < _lenS2[:, None]
        _causal = jnp.tril(jnp.ones((2048, 2048), dtype=bool))
        mask_S_fk1 = jnp.where(_validS[0], 1.0, 0.0).astype(jnp.float32)
        mask_S_fk0 = jnp.where(_validS[0], 0.0, 1.0).astype(jnp.float32)
        return (x, ctx_2048, mask_S_fk1, mask_S_fk0)
    x, ctx_2048, mask_S_fk1, mask_S_fk0 = _rec_inputs()

    def _L0_xattn_setup():
        import jax, jax.numpy as jnp
        import numpy as np
        HEADS = 16
        HEAD_DIM = 64
        SUPPRESS = 20.0
        key = jax.random.key(seed)
        ks = jax.random.split(key, 8)
        B, HW, C, T, CT = (8, 2048, 512, 77, 1024)
        inner = HEADS * HEAD_DIM
        scale = 0.02
        return {'hidden_states': jax.random.normal(ks[0], (B, HW, C), jnp.float32), 'encoder_hidden_states': jax.random.normal(ks[1], (B, T, CT), jnp.float32), 'mask_A': (jax.random.uniform(ks[2], (HW,)) > 0.5).astype(jnp.float32), 'mask_B': (jax.random.uniform(ks[3], (HW,)) > 0.5).astype(jnp.float32), 'Wq': jax.random.normal(ks[4], (C, inner), jnp.float32) * scale, 'Wk': jax.random.normal(ks[5], (CT, inner), jnp.float32) * scale, 'Wv': jax.random.normal(ks[6], (CT, inner), jnp.float32) * scale, 'Wo': jax.random.normal(ks[7], (inner, C), jnp.float32) * scale, 'bo': jnp.zeros((C,), jnp.float32), 'token_indices_A': jnp.array([2, 3], dtype=jnp.int64), 'token_indices_B': jnp.array([5, 6], dtype=jnp.int64)}
    _L0_xattn_all = _L0_xattn_setup()
    _L0_xattn_in = {k: v for k, v in _L0_xattn_all.items() if k in ('Wq', 'Wk', 'Wv', 'Wo', 'bo', 'token_indices_A', 'token_indices_B')}
    del _L0_xattn_all

    def _L1_xattn_setup():
        import jax, jax.numpy as jnp
        import numpy as np
        D_MODEL = 512
        N_HEADS = 16
        N_KV_HEADS = 4
        HEAD_DIM = D_MODEL // N_HEADS
        SPEAKER_DIM = 1024
        EPS = 1e-05

        def rmsnorm(x, w, eps=EPS):
            xf = x.astype(jnp.float32)
            inv = jax.lax.rsqrt(jnp.mean(xf * xf, axis=-1, keepdims=True) + eps)
            return (xf * inv).astype(x.dtype) * w
        key = jax.random.key(seed)
        ks = jax.random.split(key, 7)
        B, T, S = (4, 1024, 256)
        x = jax.random.normal(ks[0], (B, T, D_MODEL), dtype=jnp.float32)
        cond = jax.random.normal(ks[1], (B, S, SPEAKER_DIM), dtype=jnp.float32)
        sq = 0.02
        wq = jax.random.normal(ks[2], (D_MODEL, N_HEADS * HEAD_DIM), dtype=jnp.float32) * sq
        wk = jax.random.normal(ks[3], (SPEAKER_DIM, N_KV_HEADS * HEAD_DIM), dtype=jnp.float32) * sq
        wv = jax.random.normal(ks[4], (SPEAKER_DIM, N_KV_HEADS * HEAD_DIM), dtype=jnp.float32) * sq
        wo = jax.random.normal(ks[5], (N_HEADS * HEAD_DIM, D_MODEL), dtype=jnp.float32) * sq
        norm_w = jnp.ones((D_MODEL,), dtype=jnp.float32)
        return {'x': x, 'cond': cond, 'wq': wq, 'wk': wk, 'wv': wv, 'wo': wo, 'norm_w': norm_w}
    _L1_xattn_all = _L1_xattn_setup()
    _L1_xattn_in = {k: v for k, v in _L1_xattn_all.items() if k in ('wq', 'wk', 'wv', 'wo', 'norm_w')}
    del _L1_xattn_all

    def _L2_xattn_setup():
        import jax, jax.numpy as jnp
        import numpy as np
        HEADS = 16
        HEAD_DIM = 64
        SUPPRESS = 20.0
        key = jax.random.key(seed)
        ks = jax.random.split(key, 8)
        B, HW, C, T, CT = (8, 2048, 512, 77, 1024)
        inner = HEADS * HEAD_DIM
        scale = 0.02
        return {'hidden_states': jax.random.normal(ks[0], (B, HW, C), jnp.float32), 'encoder_hidden_states': jax.random.normal(ks[1], (B, T, CT), jnp.float32), 'mask_A': (jax.random.uniform(ks[2], (HW,)) > 0.5).astype(jnp.float32), 'mask_B': (jax.random.uniform(ks[3], (HW,)) > 0.5).astype(jnp.float32), 'Wq': jax.random.normal(ks[4], (C, inner), jnp.float32) * scale, 'Wk': jax.random.normal(ks[5], (CT, inner), jnp.float32) * scale, 'Wv': jax.random.normal(ks[6], (CT, inner), jnp.float32) * scale, 'Wo': jax.random.normal(ks[7], (inner, C), jnp.float32) * scale, 'bo': jnp.zeros((C,), jnp.float32), 'token_indices_A': jnp.array([2, 3], dtype=jnp.int64), 'token_indices_B': jnp.array([5, 6], dtype=jnp.int64)}
    _L2_xattn_all = _L2_xattn_setup()
    _L2_xattn_in = {k: v for k, v in _L2_xattn_all.items() if k in ('Wq', 'Wk', 'Wv', 'Wo', 'bo', 'token_indices_A', 'token_indices_B')}
    del _L2_xattn_all

    def _L3_xattn_setup():
        import jax, jax.numpy as jnp
        import numpy as np
        D_MODEL = 512
        N_HEADS = 16
        N_KV_HEADS = 4
        HEAD_DIM = D_MODEL // N_HEADS
        SPEAKER_DIM = 1024
        EPS = 1e-05

        def rmsnorm(x, w, eps=EPS):
            xf = x.astype(jnp.float32)
            inv = jax.lax.rsqrt(jnp.mean(xf * xf, axis=-1, keepdims=True) + eps)
            return (xf * inv).astype(x.dtype) * w
        key = jax.random.key(seed)
        ks = jax.random.split(key, 7)
        B, T, S = (4, 1024, 256)
        x = jax.random.normal(ks[0], (B, T, D_MODEL), dtype=jnp.float32)
        cond = jax.random.normal(ks[1], (B, S, SPEAKER_DIM), dtype=jnp.float32)
        sq = 0.02
        wq = jax.random.normal(ks[2], (D_MODEL, N_HEADS * HEAD_DIM), dtype=jnp.float32) * sq
        wk = jax.random.normal(ks[3], (SPEAKER_DIM, N_KV_HEADS * HEAD_DIM), dtype=jnp.float32) * sq
        wv = jax.random.normal(ks[4], (SPEAKER_DIM, N_KV_HEADS * HEAD_DIM), dtype=jnp.float32) * sq
        wo = jax.random.normal(ks[5], (N_HEADS * HEAD_DIM, D_MODEL), dtype=jnp.float32) * sq
        norm_w = jnp.ones((D_MODEL,), dtype=jnp.float32)
        return {'x': x, 'cond': cond, 'wq': wq, 'wk': wk, 'wv': wv, 'wo': wo, 'norm_w': norm_w}
    _L3_xattn_all = _L3_xattn_setup()
    _L3_xattn_in = {k: v for k, v in _L3_xattn_all.items() if k in ('wq', 'wk', 'wv', 'wo', 'norm_w')}
    del _L3_xattn_all
    return {'x': x, 'ctx_2048': ctx_2048, 'mask_S_fk1': mask_S_fk1, 'mask_S_fk0': mask_S_fk0, 'L0_xattn_Wq': _L0_xattn_in['Wq'], 'L0_xattn_Wk': _L0_xattn_in['Wk'], 'L0_xattn_Wv': _L0_xattn_in['Wv'], 'L0_xattn_Wo': _L0_xattn_in['Wo'], 'L0_xattn_bo': _L0_xattn_in['bo'], 'L0_xattn_token_indices_A': _L0_xattn_in['token_indices_A'], 'L0_xattn_token_indices_B': _L0_xattn_in['token_indices_B'], 'L1_xattn_wq': _L1_xattn_in['wq'], 'L1_xattn_wk': _L1_xattn_in['wk'], 'L1_xattn_wv': _L1_xattn_in['wv'], 'L1_xattn_wo': _L1_xattn_in['wo'], 'L1_xattn_norm_w': _L1_xattn_in['norm_w'], 'L2_xattn_Wq': _L2_xattn_in['Wq'], 'L2_xattn_Wk': _L2_xattn_in['Wk'], 'L2_xattn_Wv': _L2_xattn_in['Wv'], 'L2_xattn_Wo': _L2_xattn_in['Wo'], 'L2_xattn_bo': _L2_xattn_in['bo'], 'L2_xattn_token_indices_A': _L2_xattn_in['token_indices_A'], 'L2_xattn_token_indices_B': _L2_xattn_in['token_indices_B'], 'L3_xattn_wq': _L3_xattn_in['wq'], 'L3_xattn_wk': _L3_xattn_in['wk'], 'L3_xattn_wv': _L3_xattn_in['wv'], 'L3_xattn_wo': _L3_xattn_in['wo'], 'L3_xattn_norm_w': _L3_xattn_in['norm_w']}

def reference(x, ctx_2048, mask_S_fk1, mask_S_fk0, L0_xattn_Wq, L0_xattn_Wk, L0_xattn_Wv, L0_xattn_Wo, L0_xattn_bo, L0_xattn_token_indices_A, L0_xattn_token_indices_B, L1_xattn_wq, L1_xattn_wk, L1_xattn_wv, L1_xattn_wo, L1_xattn_norm_w, L2_xattn_Wq, L2_xattn_Wk, L2_xattn_Wv, L2_xattn_Wo, L2_xattn_bo, L2_xattn_token_indices_A, L2_xattn_token_indices_B, L3_xattn_wq, L3_xattn_wk, L3_xattn_wv, L3_xattn_wo, L3_xattn_norm_w):
    import jax
    import jax.numpy as jnp

    def _L0_xattn_ref(hidden_states, encoder_hidden_states, mask_A, mask_B, Wq, Wk, Wv, Wo, bo, token_indices_A, token_indices_B):
        import jax, jax.numpy as jnp
        import numpy as np
        HEADS = 16
        HEAD_DIM = 64
        SUPPRESS = 20.0
        B, HW, C = hidden_states.shape
        T = encoder_hidden_states.shape[1]
        residual = hidden_states
        q = hidden_states @ Wq
        k = encoder_hidden_states @ Wk
        v = encoder_hidden_states @ Wv
        q = q.reshape(B, HW, HEADS, HEAD_DIM).transpose(0, 2, 1, 3)
        k = k.reshape(B, T, HEADS, HEAD_DIM).transpose(0, 2, 1, 3)
        v = v.reshape(B, T, HEADS, HEAD_DIM).transpose(0, 2, 1, 3)
        scale = HEAD_DIM ** (-0.5)
        logits = jnp.einsum('bhqd,bhkd->bhqk', q, k) * scale
        suppress_A_in = 1.0 - mask_A
        suppress_B_in = 1.0 - mask_B
        col_bias = jnp.zeros((HW, T), logits.dtype)
        col_bias = col_bias.at[:, token_indices_A].set((-SUPPRESS * suppress_A_in)[:, None])
        col_bias = col_bias.at[:, token_indices_B].set((-SUPPRESS * suppress_B_in)[:, None])
        logits = logits + col_bias[None, None, :, :]
        probs = jax.nn.softmax(logits, axis=-1)
        out = jnp.einsum('bhqk,bhkd->bhqd', probs, v)
        out = out.transpose(0, 2, 1, 3).reshape(B, HW, HEADS * HEAD_DIM)
        out = out @ Wo + bo
        out = out + residual
        return out

    def _L1_xattn_ref(x, cond, wq, wk, wv, wo, norm_w):
        import jax, jax.numpy as jnp
        import numpy as np
        D_MODEL = 512
        N_HEADS = 16
        N_KV_HEADS = 4
        HEAD_DIM = D_MODEL // N_HEADS
        SPEAKER_DIM = 1024
        EPS = 1e-05

        def rmsnorm(x, w, eps=EPS):
            xf = x.astype(jnp.float32)
            inv = jax.lax.rsqrt(jnp.mean(xf * xf, axis=-1, keepdims=True) + eps)
            return (xf * inv).astype(x.dtype) * w
        B, T, _ = x.shape
        S = cond.shape[1]
        n_rep = N_HEADS // N_KV_HEADS
        residual = x
        xn = rmsnorm(x, norm_w)
        q = (xn @ wq).reshape(B, T, N_HEADS, HEAD_DIM)
        k = (cond @ wk).reshape(B, S, N_KV_HEADS, HEAD_DIM)
        v = (cond @ wv).reshape(B, S, N_KV_HEADS, HEAD_DIM)
        qg = q.reshape(B, T, N_KV_HEADS, n_rep, HEAD_DIM)
        scale = 1.0 / np.sqrt(HEAD_DIM).astype(np.float32)
        scores = jnp.einsum('btgrd,bsgd->bgrts', qg, k) * scale
        attn = jax.nn.softmax(scores.astype(jnp.float32), axis=-1).astype(q.dtype)
        out = jnp.einsum('bgrts,bsgd->btgrd', attn, v).reshape(B, T, N_HEADS * HEAD_DIM)
        return residual + out @ wo

    def _L2_xattn_ref(hidden_states, encoder_hidden_states, mask_A, mask_B, Wq, Wk, Wv, Wo, bo, token_indices_A, token_indices_B):
        import jax, jax.numpy as jnp
        import numpy as np
        HEADS = 16
        HEAD_DIM = 64
        SUPPRESS = 20.0
        B, HW, C = hidden_states.shape
        T = encoder_hidden_states.shape[1]
        residual = hidden_states
        q = hidden_states @ Wq
        k = encoder_hidden_states @ Wk
        v = encoder_hidden_states @ Wv
        q = q.reshape(B, HW, HEADS, HEAD_DIM).transpose(0, 2, 1, 3)
        k = k.reshape(B, T, HEADS, HEAD_DIM).transpose(0, 2, 1, 3)
        v = v.reshape(B, T, HEADS, HEAD_DIM).transpose(0, 2, 1, 3)
        scale = HEAD_DIM ** (-0.5)
        logits = jnp.einsum('bhqd,bhkd->bhqk', q, k) * scale
        suppress_A_in = 1.0 - mask_A
        suppress_B_in = 1.0 - mask_B
        col_bias = jnp.zeros((HW, T), logits.dtype)
        col_bias = col_bias.at[:, token_indices_A].set((-SUPPRESS * suppress_A_in)[:, None])
        col_bias = col_bias.at[:, token_indices_B].set((-SUPPRESS * suppress_B_in)[:, None])
        logits = logits + col_bias[None, None, :, :]
        probs = jax.nn.softmax(logits, axis=-1)
        out = jnp.einsum('bhqk,bhkd->bhqd', probs, v)
        out = out.transpose(0, 2, 1, 3).reshape(B, HW, HEADS * HEAD_DIM)
        out = out @ Wo + bo
        out = out + residual
        return out

    def _L3_xattn_ref(x, cond, wq, wk, wv, wo, norm_w):
        import jax, jax.numpy as jnp
        import numpy as np
        D_MODEL = 512
        N_HEADS = 16
        N_KV_HEADS = 4
        HEAD_DIM = D_MODEL // N_HEADS
        SPEAKER_DIM = 1024
        EPS = 1e-05

        def rmsnorm(x, w, eps=EPS):
            xf = x.astype(jnp.float32)
            inv = jax.lax.rsqrt(jnp.mean(xf * xf, axis=-1, keepdims=True) + eps)
            return (xf * inv).astype(x.dtype) * w
        B, T, _ = x.shape
        S = cond.shape[1]
        n_rep = N_HEADS // N_KV_HEADS
        residual = x
        xn = rmsnorm(x, norm_w)
        q = (xn @ wq).reshape(B, T, N_HEADS, HEAD_DIM)
        k = (cond @ wk).reshape(B, S, N_KV_HEADS, HEAD_DIM)
        v = (cond @ wv).reshape(B, S, N_KV_HEADS, HEAD_DIM)
        qg = q.reshape(B, T, N_KV_HEADS, n_rep, HEAD_DIM)
        scale = 1.0 / np.sqrt(HEAD_DIM).astype(np.float32)
        scores = jnp.einsum('btgrd,bsgd->bgrts', qg, k) * scale
        attn = jax.nn.softmax(scores.astype(jnp.float32), axis=-1).astype(q.dtype)
        out = jnp.einsum('bgrts,bsgd->btgrd', attn, v).reshape(B, T, N_HEADS * HEAD_DIM)
        return residual + out @ wo
    x = _L0_xattn_ref(x, ctx_2048, mask_S_fk1, mask_S_fk0, L0_xattn_Wq, L0_xattn_Wk, L0_xattn_Wv, L0_xattn_Wo, L0_xattn_bo, L0_xattn_token_indices_A, L0_xattn_token_indices_B)
    x = _L1_xattn_ref(x, ctx_2048, L1_xattn_wq, L1_xattn_wk, L1_xattn_wv, L1_xattn_wo, L1_xattn_norm_w)
    x = _L2_xattn_ref(x, ctx_2048, mask_S_fk1, mask_S_fk0, L2_xattn_Wq, L2_xattn_Wk, L2_xattn_Wv, L2_xattn_Wo, L2_xattn_bo, L2_xattn_token_indices_A, L2_xattn_token_indices_B)
    x = _L3_xattn_ref(x, ctx_2048, L3_xattn_wq, L3_xattn_wk, L3_xattn_wv, L3_xattn_wo, L3_xattn_norm_w)
    return x

_drawn_inputs = setup_inputs


def setup_inputs(seed=0):
    import zlib

    import numpy as np

    out = dict(_drawn_inputs(seed))
    spreads = {'L0_xattn_bo': (0.0, 0.1),
     'L1_xattn_norm_w': (1.0, 0.6),
     'L2_xattn_bo': (0.0, 0.1),
     'L3_xattn_norm_w': (1.0, 0.6)}
    factors = {'mask_S_fk1': 8.0,
     'mask_S_fk0': 8.0,
     'L0_xattn_Wq': 2.79,
     'L0_xattn_Wk': 2.761,
     'L1_xattn_wq': 3.615,
     'L1_xattn_wk': 3.605,
     'L2_xattn_Wq': 2.694,
     'L2_xattn_Wk': 2.686,
     'L3_xattn_wq': 3.593,
     'L3_xattn_wk': 3.652}
    for name, (base, spread) in spreads.items():
        noise = np.random.default_rng([zlib.crc32(name.encode()), seed]).standard_normal(out[name].shape)
        drawn = base * np.exp(spread * noise) if base else spread * noise
        out[name] = jnp.asarray(drawn.astype(out[name].dtype))
    for name, factor in factors.items():
        out[name] = (out[name] * factor).astype(out[name].dtype)
    return out
```

```python
from contextlib import ExitStack

import numpy as np
import concourse.bass as bass
from concourse import mybir

ALU = mybir.AluOpType
ACT = mybir.ActivationFunctionType
X = mybir.AxisListType.X
F32 = mybir.dt.float32
F32R = mybir.dt.float32r
I32 = mybir.dt.int32

P = 128
ROUNDS = 2
BATCH, ROWS, C = 2, 2048, 512
TOK, CTX = 77, 1024
HEADS = 16
DENSE_D, GROUP_D, KV_HEADS = 64, 32, 4
INNER = HEADS * DENSE_D
KEYS = HEADS * TOK
TILES = ROWS // P
CT, XT = C // P, CTX // P
PAIRS = INNER // P
CHUNKS = -(-KEYS // P)
BANK = 512
UNROLL = 2
ALIKE = (3, TILES - 3)
GV = GROUP_D + 2
EPS = 1e-5
SUPPRESS = 20.0
DENSE_SCALE = DENSE_D ** -0.5
GROUP_SCALE = float(np.float32(1.0) / np.sqrt(GROUP_D).astype(np.float32))

S_BANKS = [(0, 6), (6, 6), (12, 4)]
T_BANKS = [(0, 4), (4, 4), (8, 2)]


def rows_of(c):
    return min(P, KEYS - c * P)


def heads_of(c):
    return range(c * P // TOK, (c * P + rows_of(c) - 1) // TOK + 1)


def pairs_of(c):
    return range(c * P // (2 * TOK), (c * P + rows_of(c) - 1) // (2 * TOK) + 1)


SLOT = [sum(len(heads_of(b)) for b in range(c)) for c in range(CHUNKS + 1)]
SLOTS = SLOT[CHUNKS]
WINDOW = 3 * P


def window_start(p):
    return p * 2 * TOK // P * P


def build(nc, x, ctx_t, mask_a, mask_b, d_wq_t, d_wk, d_wv, d_wo, d_bo, d_idx,
          g_wq, g_wk, g_wv, g_wo, g_norm, ident_c, half_c, quarter_c, member_c, select_c, spread_c, token_c, out):
    ctx = ExitStack()
    with ctx:
        def sem(name):
            return ctx.enter_context(nc.semaphore(name))

        def sb(name, shape, dt=F32, scope=ctx):
            return scope.enter_context(nc.sbuf_tensor(name, shape, dt))

        ident = sb("ident", [P, P])
        half = sb("half", [P, 2])
        quarter = sb("quarter", [P, 4])
        member = sb("member", [P, SLOTS])
        ctx_sb = sb("ctx_sb", [P, XT, BATCH * TOK])
        x_ring = sb("x_ring", [P, TILES, C])
        wst = [sb(f"wst{n}", [P, XT, C]) for n in range(2)]
        small = sb("small", [P, 64])
        banks = ctx.enter_context(nc.psum_tensor("banks", [P, 8, BANK], F32))

        with ExitStack() as s:
            kt_hi = sb("kt_hi", [P, CT, KEYS], F32R, s)
            kt_lo = sb("kt_lo", [P, CT, KEYS], F32R, s)
            vt_hi = sb("vt_hi", [P, CHUNKS, C], F32R, s)
            vt_lo = sb("vt_lo", [P, CHUNKS, C], F32R, s)
        with ExitStack() as s:
            gq_hi = sb("gq_hi", [P, CT, C], F32R, s)
            gq_lo = sb("gq_lo", [P, CT, C], F32R, s)
            go_hi = sb("go_hi", [P, CT, C], F32R, s)
            go_lo = sb("go_lo", [P, CT, C], F32R, s)
            gk_hi = sb("gk_hi", [P, KV_HEADS, BATCH, 4 * TOK], F32R, s)
            gk_lo = sb("gk_lo", [P, KV_HEADS, BATCH, 4 * TOK], F32R, s)
            gv_hi = sb("gv_hi", [P, BATCH, SLOTS, GV], F32R, s)
            gv_lo = sb("gv_lo", [P, BATCH, SLOTS, GV], F32R, s)
        sb("tables_place", [P, 2 * CT * KEYS + 2 * CHUNKS * C])

        with ExitStack() as s:
            bias8 = sb("bias8", [P, TILES, TOK], F32, s)
            bo_sb = sb("bo_sb", [P, C], F32, s)
            k_t = sb("k_t", [P, PAIRS, BATCH * TOK], F32, s)
            v_t = sb("v_t", [P, PAIRS, BATCH * TOK], F32, s)
        with ExitStack() as s:
            q_sb = sb("q_sb", [P, C], F32, s)
            qt_hi = sb("qt_hi", [P, 2, CT, P], F32R, s)
            qt_lo = sb("qt_lo", [P, 2, CT, P], F32R, s)
            o_sb = sb("o_sb", [P, C], F32, s)
            ot_hi = sb("ot_hi", [P, CT, P], F32R, s)
            ot_lo = sb("ot_lo", [P, CT, P], F32R, s)
            xn = sb("xn", [P, C], F32, s)
            squares = sb("squares", [P, C], mybir.dt.bfloat16, s)
        sb("layer_place", [P, 19 * C // 2 + 64])

        with ExitStack() as s:
            xt_hi = sb("xt_hi", [P, 2, CT, P], F32R, s)
            xt_lo = sb("xt_lo", [P, 2, CT, P], F32R, s)
            pt_hi = sb("pt_hi", [P, CHUNKS, P], F32R, s)
            pt_lo = sb("pt_lo", [P, CHUNKS, P], F32R, s)
            probs = sb("probs", [P, 2, KEYS], F32, s)
            xs = sb("xs", [P, 2, C], F32, s)
        with ExitStack() as s:
            k_bd = sb("k_bd", [P, PAIRS, 2 * TOK], F32, s)
            v_bd = sb("v_bd", [P, PAIRS, WINDOW], F32, s)
            tok_sb = sb("tok_sb", [P, TOK], F32, s)
            idx_i = sb("idx_i", [P, 4], I32, s)
            idx_f = sb("idx_f", [P, 8], F32, s)
            hot = sb("hot", [P, 8, TOK], F32, s)
            bias_b = sb("bias_b", [P, TILES, TOK], F32, s)
            m_sb = sb("m_sb", [P, 2, TILES], F32, s)
        with ExitStack() as s:
            gk_raw = sb("gk_raw", [P, BATCH, 4 * TOK], F32, s)
            gq_raw = sb("gq_raw", [P, CT, C], F32, s)
            gv_raw = sb("gv_raw", [P, SLOTS, GV], F32, s)
            k1 = sb("k1", [P, BATCH * TOK], F32, s)
            v1 = sb("v1", [P, BATCH, P], F32, s)
            spread = sb("spread", [P, KV_HEADS * P], F32, s)
            select = sb("select", [TOK, KEYS], F32, s)
            norm_sb = sb("norm_sb", [P, CT], F32, s)
        sb("work_place", [P, 16 * P + 2 * CHUNKS * P + 2 * KEYS + 2 * C + 64])

        row_max = small[:, 0:16]
        row_sum = small[:, 16:32]
        row_rcp = small[:, 32:48]
        ssq = small[:, 48:49]
        rms = small[:, 49:50]
        mean_sq = small[:, 50:51]
        exponent = small[:, 51:52]

        x_mid = nc.dram_tensor("x_mid", [BATCH, TILES, P, C], F32, kind="Internal").ap()

        const_in = sem("const_in")
        passed = sem("passed")
        stage_done = sem("stage_done")
        x_in = [sem(f"x_in{i}") for i in range(TILES)]
        x_out = [sem(f"x_out{i}") for i in range(TILES)]
        xs_ready = sem("xs_ready")
        x_updated = sem("x_updated")
        w_in = [sem("w_in0"), sem("w_in1")]
        gw_in = sem("gw_in")
        aux_in = sem("aux_in")
        proj_done, proj_read = sem("proj_done"), sem("proj_read")
        bd_ready, zero_done = sem("bd_ready"), sem("zero_done")
        tab_done, tab_hi, tab_lo = sem("tab_done"), sem("tab_hi"), sem("tab_lo")
        bias_link = sem("bias_link")
        d_xt_raw, d_xt_hi, d_xt_lo = sem("d_xt_raw"), sem("d_xt_hi"), sem("d_xt_lo")
        d_scores, d_biased, d_max = sem("d_scores"), sem("d_biased"), sem("d_max")
        d_shifted, d_exp, d_sum, d_rcp = sem("d_shifted"), sem("d_exp"), sem("d_sum"), sem("d_rcp")
        d_probs, d_bo_added = sem("d_probs"), sem("d_bo_added")
        d_pt_raw, d_pt_hi, d_pt_lo = sem("d_pt_raw"), sem("d_pt_hi"), sem("d_pt_lo")
        d_out = sem("d_out")
        g_proj, g_built, g_spread = sem("g_proj"), sem("g_built"), sem("g_spread")
        g_rep, g_rep_read = sem("g_rep"), sem("g_rep_read")
        g_raw, g_hi, g_lo, g_cleared = sem("g_raw"), sem("g_hi"), sem("g_lo"), sem("g_cleared")
        exponent_set = sem("exponent_set")
        g_sq, g_var, g_rms, g_xn = sem("g_sq"), sem("g_var"), sem("g_rms"), sem("g_xn")
        g_xt_raw, g_xt_hi, g_xt_lo = sem("g_xt_raw"), sem("g_xt_hi"), sem("g_xt_lo")
        g_q, g_q_sb = sem("g_q"), sem("g_q_sb")
        g_qt_raw, g_qt_hi, g_qt_lo = sem("g_qt_raw"), sem("g_qt_hi"), sem("g_qt_lo")
        g_scores, g_max, g_shifted, g_exp = sem("g_scores"), sem("g_max"), sem("g_shifted"), sem("g_exp")
        g_pt_raw, g_pt_hi, g_pt_lo = sem("g_pt_raw"), sem("g_pt_hi"), sem("g_pt_lo")
        g_o, g_rcp, g_o_sb = sem("g_o"), sem("g_rcp"), sem("g_o_sb")
        g_ot_raw, g_ot_hi, g_ot_lo = sem("g_ot_raw"), sem("g_ot_hi"), sem("g_ot_lo")
        g_out = sem("g_out")

        STAGES = 8

        def stage_end(eng, rnd, n):
            eng.drain().then_inc(stage_done, 1)
            eng.wait_ge(stage_done, 4 * STAGES * rnd + 4 * (n + 1))
            eng.sem_inc(passed, 1)

        def sweep(eng, first, last, step):
            for i in range(first, ALIKE[0]):
                step(i, i)
            with eng.Fori(0, (ALIKE[1] - ALIKE[0]) // UNROLL) as j:
                for u in range(UNROLL):
                    step(UNROLL * j + (ALIKE[0] + u), ALIKE[0] + u)
            for i in range(ALIKE[1], last + 1):
                step(i, i)

        def there(i, d, lo=0):
            return not isinstance(i, int) or lo <= i + d < TILES

        def product(pe, dst, pairs, first=True, last=True, check=True):
            n = 3 * len(pairs)
            at = 0
            for (a_hi, a_lo), (b_hi, b_lo) in pairs:
                for a, b in ((a_hi, b_hi), (a_hi, b_lo), (a_lo, b_hi)):
                    mm = pe.matmul(dst, a, b, start=first and at == 0, stop=last and at == n - 1,
                                   skip_group_check=not check)
                    at += 1
            return mm

        GROUPS = CT * len(S_BANKS) + CHUNKS

        def dense_tables_pe(pe, rnd, b):
            base = (rnd * BATCH + b) * GROUPS
            pe.wait_ge(w_in[0], 48 * rnd + 48)
            pe.wait_ge(bd_ready, (rnd * BATCH + b) * 9 + 1)
            n = 0
            for ct in range(CT):
                for k, (h0, nh) in enumerate(S_BANKS):
                    if n >= 8:
                        pe.wait_ge(tab_lo, base + n - 7)
                    for p in range(h0 // 2, (h0 + nh) // 2):
                        at = (p - h0 // 2) * 2 * TOK
                        mm = pe.matmul(banks[:, n % 8, at:at + 2 * TOK], wst[0][:, p, ct * P:(ct + 1) * P],
                                       k_bd[:, p, :], start=True, stop=True)
                    mm.then_inc(tab_done, 1)
                    n += 1
            pe.wait_ge(w_in[1], 48 * rnd + 48)
            pe.wait_ge(bd_ready, (rnd * BATCH + b) * 9 + 9)
            for c in range(CHUNKS):
                pe.wait_ge(tab_lo, base + n - 7)
                for p in pairs_of(c):
                    at = c * P - window_start(p)
                    mm = pe.matmul(banks[0:rows_of(c), n % 8, :], v_bd[:, p, at:at + rows_of(c)], wst[1][:, p, :],
                                   start=p == pairs_of(c)[0], stop=p == pairs_of(c)[-1])
                mm.then_inc(tab_done, 1)
                n += 1

        def dense_tiles_pe(pe, g0, a0):
            def turn_x(i, u):
                pe.wait_ge(xs_ready, a0 + i + 1)
                for ct in range(CT):
                    mm = pe.transpose(banks[:, 6, ct * P:(ct + 1) * P], xs[:, u % 2, ct * P:(ct + 1) * P], ident[:, :])
                mm.then_inc(d_xt_raw, 1)

            def step(i, u):
                g = g0 + i
                if there(i, -2):
                    pe.wait_ge(d_probs, g - 1)
                    for k, (c0, ncs) in enumerate(T_BANKS):
                        if there(i, -3):
                            pe.wait_ge(d_pt_lo, 3 * g - 8 + k)
                        for c in range(c0, c0 + ncs):
                            mm = pe.transpose(banks[0:rows_of(c), 3 + k, (c - c0) * P:(c - c0 + 1) * P],
                                              probs[:, u % 2, c * P:c * P + rows_of(c)], ident[:, :])
                        mm.then_inc(d_pt_raw, 1)
                if isinstance(i, int) and i == 0:
                    turn_x(0, 0)
                if there(i, 0):
                    pe.wait_ge(d_xt_lo, g + 1)
                    for k, (h0, nh) in enumerate(S_BANKS):
                        if there(i, -1):
                            pe.wait_ge(d_biased, 3 * g - 2 + k)
                        cols = slice(h0 * TOK, (h0 + nh) * TOK)
                        product(pe, banks[:, k, 0:nh * TOK],
                                [((xt_hi[:, u % 2, ct, :], xt_lo[:, u % 2, ct, :]), (kt_hi[:, ct, cols], kt_lo[:, ct, cols]))
                                 for ct in range(CT)]).then_inc(d_scores, 1)
                if there(i, 1, 1):
                    turn_x(i + 1, u + 1)
                if there(i, -2):
                    if there(i, -3):
                        pe.wait_ge(x_updated, a0 + i - 2)
                    for c in range(CHUNKS):
                        if c % 4 == 0:
                            pe.wait_ge(d_pt_lo, 3 * g - 5 + c // 4)
                        r = rows_of(c)
                        mm = product(pe, banks[:, 7, :], [((pt_hi[0:r, c, :], pt_lo[0:r, c, :]), (vt_hi[0:r, c, :], vt_lo[0:r, c, :]))],
                                     first=c == 0, last=c == CHUNKS - 1)
                    mm.then_inc(d_out, 1)

            sweep(pe, 0, TILES + 1, step)

        def group_tables_pe(pe, rnd):
            pe.wait_ge(gw_in, 112 * rnd + 112)
            wk = wst[0][:, 0:2, :].rearrange("p a n -> p (a n)").rearrange("p (t n) -> p t n", t=XT)
            wv = wst[0][:, 2:4, :].rearrange("p a n -> p (a n)").rearrange("p (t n) -> p t n", t=XT)
            for kt in range(XT):
                mm = pe.matmul(banks[:, 0, 0:BATCH * TOK], wk[:, kt, :], ctx_sb[:, kt, :], start=kt == 0, stop=kt == XT - 1)
            mm.then_inc(g_proj, 1)
            for b in range(BATCH):
                for kt in range(XT):
                    mm = pe.matmul(banks[0:TOK, 4 + b, 0:P], ctx_sb[:, kt, b * TOK:(b + 1) * TOK], wv[:, kt, :],
                                   start=kt == 0, stop=kt == XT - 1)
                mm.then_inc(g_proj, 1)
            pe.wait_ge(g_built, 3 * rnd + 1)
            for g in range(KV_HEADS):
                pe.matmul(banks[:, g, 0:BATCH * TOK], spread[:, g * P:(g + 1) * P], k1[:, :],
                          start=True, stop=True).then_inc(g_spread, 1)
            pe.wait_ge(g_built, 3 * rnd + 3)
            n = 0
            for b in range(BATCH):
                for c in range(CHUNKS):
                    if n >= 2:
                        pe.wait_ge(g_rep_read, BATCH * CHUNKS * rnd + n - 1)
                    r = rows_of(c)
                    pe.matmul(banks[0:r, 6 + n % 2, 0:P], select[:, c * P:c * P + r], v1[0:TOK, b, :],
                              start=True, stop=True).then_inc(g_rep, 1)
                    n += 1

        def group_tiles_pe(pe, b, g0, a0):
            def step(i, u):
                g = g0 + i

                def turn_probs(k, bank):
                    c0, ncs = T_BANKS[k]
                    for c in range(c0, c0 + ncs):
                        mm = pe.transpose(banks[0:rows_of(c), bank, (c - c0) * P:(c - c0 + 1) * P],
                                          probs[:, u % 2, c * P:c * P + rows_of(c)], ident[:, :])
                    mm.then_inc(g_pt_raw, 1)

                def scores(k):
                    h0, nh = S_BANKS[k]
                    if k == 0:
                        pe.wait_ge(g_qt_lo, g + 1)
                    if there(i, -1):
                        pe.wait_ge(g_shifted, 3 * g - 2 + k)
                    for grp in range(h0 // 4, -(-(h0 + nh) // 4)):
                        lo, hi = max(h0, 4 * grp), min(h0 + nh, 4 * grp + 4)
                        cols = slice((lo - 4 * grp) * TOK, (hi - 4 * grp) * TOK)
                        mm = product(pe, banks[:, k, (lo - h0) * TOK:(hi - h0) * TOK],
                                     [((qt_hi[:, u % 2, grp, :], qt_lo[:, u % 2, grp, :]),
                                       (gk_hi[:, grp, b, cols], gk_lo[:, grp, b, cols]))])
                    mm.then_inc(g_scores, 1)

                if there(i, -2):
                    pe.wait_ge(g_exp, g - 1)
                    if there(i, -3):
                        pe.wait_ge(g_pt_lo, 3 * g - 6)
                    turn_probs(0, 3)
                    turn_probs(1, 4)
                if there(i, 1):
                    pe.wait_ge(g_xn, g + 2)
                    if there(i, -3):
                        pe.wait_ge(g_ot_lo, g - 2)
                    elif there(i, 0):
                        pe.wait_ge(g_qt_lo, g + 1)
                    for ct in range(CT):
                        mm = pe.transpose(banks[:, 5, ct * P:(ct + 1) * P], xn[:, ct * P:(ct + 1) * P], ident[:, :])
                    mm.then_inc(g_xt_raw, 1)
                if there(i, -3):
                    pe.wait_ge(g_ot_lo, g - 2)
                    product(pe, banks[:, 6, :], [((ot_hi[:, ct, :], ot_lo[:, ct, :]), (go_hi[:, ct, :], go_lo[:, ct, :]))
                                                 for ct in range(CT)]).then_inc(g_out, 1)
                if there(i, -2):
                    pe.wait_ge(g_pt_lo, 3 * g - 5)
                    turn_probs(2, 3)
                if there(i, 0):
                    scores(0)
                if there(i, 1):
                    pe.wait_ge(g_xt_lo, g + 2)
                    product(pe, banks[:, 7, :], [((xt_hi[:, 0, ct, :], xt_lo[:, 0, ct, :]), (gq_hi[:, ct, :], gq_lo[:, ct, :]))
                                                 for ct in range(CT)]).then_inc(g_q, 1)
                if there(i, 0):
                    scores(1)
                if there(i, -2):
                    if there(i, -3):
                        pe.wait_ge(x_updated, a0 + i - 2)
                    if there(i, 1):
                        pe.wait_ge(g_q_sb, g + 2)
                    for c in range(CHUNKS):
                        if c % 4 == 0:
                            pe.wait_ge(g_pt_lo, 3 * g - 5 + c // 4)
                        r = rows_of(c)
                        for side in range(2):
                            hs = [h for h in heads_of(c) if h // 8 == side]
                            if not hs:
                                continue
                            s0 = SLOT[c] + hs[0] - heads_of(c)[0]
                            new = c == 0 or (side == 1 and hs[0] == 8 and c == 8 * TOK // P)
                            at = (hs[0] - 8 * side) * GV
                            mm = product(pe, banks[:, 6 + side, at:at + len(hs) * GV],
                                         [((pt_hi[0:r, c, :], pt_lo[0:r, c, :]),
                                           (gv_hi[0:r, b, s0:s0 + len(hs), :], gv_lo[0:r, b, s0:s0 + len(hs), :]))],
                                         first=new, last=c == CHUNKS - 1, check=False)
                    mm.then_inc(g_o, 1)
                if there(i, 1):
                    pe.wait_ge(g_q_sb, g + 2)
                    for ct in range(CT):
                        mm = pe.transpose(banks[:, 5, ct * P:(ct + 1) * P], q_sb[:, ct * P:(ct + 1) * P], ident[:, :])
                    mm.then_inc(g_qt_raw, 1)
                if there(i, 0):
                    scores(2)
                if there(i, -2):
                    pe.wait_ge(g_o_sb, 2 * g - 2)
                    if there(i, 1):
                        pe.wait_ge(g_qt_lo, g + 2)
                    for ct in range(CT):
                        mm = pe.transpose(banks[:, 5, ct * P:(ct + 1) * P], o_sb[:, ct * P:(ct + 1) * P], ident[:, :])
                    mm.then_inc(g_ot_raw, 1)

            sweep(pe, -1, TILES + 2, step)

        def of_round(w, rnd):
            return w[bass.ds(rnd, 1)].rearrange("r (t p) n -> p (r t) n", p=P)

        def dense_project_act(act, rnd):
            parts = [of_round(w, rnd)[:, :, q * C:(q + 1) * C] for w in (d_wk, d_wv) for q in range(2)]
            parts += [of_round(d_wq_t, rnd), of_round(d_wo, rnd)]
            act.dma_start(wst[0][:, :, :], parts[0]).then_inc(w_in[0], 16)
            act.dma_start(wst[1][:, :, :], parts[1]).then_inc(w_in[1], 16)
            for dst, src in ((tok_sb, token_c), (idx_i, d_idx[bass.ds(rnd, 1)].rearrange("r p n -> p (r n)")),
                             (m_sb[:, 0, :], mask_a), (m_sb[:, 1, :], mask_b),
                             (bo_sb, d_bo[bass.ds(rnd, 1)].rearrange("r p n -> p (r n)"))):
                act.dma_start(dst[:, :], src).then_inc(aux_in, 16)
            for n in range(4):
                for t in range(4 * n, 4 * n + 4):
                    act.wait_ge(proj_done, 16 * rnd + t + 1)
                    act.activation((k_t if t < PAIRS else v_t)[:, t % PAIRS, :], banks[:, t % 8, 0:BATCH * TOK],
                                   ACT.Copy).then_inc(proj_read, 1)
                act.dma_start(wst[n % 2][:, :, :], parts[n + 2]).then_inc(w_in[n % 2], 16)

        def dense_tiles_act(act, g0):
            def xt_part(i, u):
                act.wait_ge(d_xt_raw, g0 + i + 1)
                if there(i, -2):
                    act.wait_ge(d_scores, 3 * (g0 + i) - 3)
                act.activation(xt_hi[:, u % 2, :, :].rearrange("p t n -> p (t n)"), banks[:, 6, :],
                               ACT.Copy).then_inc(d_xt_hi, 1)

            def step(i, u):
                g = g0 + i
                if there(i, -2):
                    if there(i, -3):
                        act.wait_ge(d_out, g - 2)
                    for k, (c0, ncs) in enumerate(T_BANKS):
                        act.wait_ge(d_pt_raw, 3 * g - 5 + k)
                        copy_probs(act, k, 3 + k).then_inc(d_pt_hi, 1)
                if isinstance(i, int) and i == 0:
                    xt_part(0, 0)
                if there(i, 1, 1):
                    xt_part(i + 1, u + 1)
                if there(i, 0):
                    act.wait_ge(d_shifted, g + 1)
                    act.activation(probs[:, u % 2, :], probs[:, u % 2, :], ACT.Exp, scale=DENSE_SCALE).then_inc(d_exp, 1)

            sweep(act, 0, TILES + 1, step)

        def copy_probs(act, k, bank):
            c0, ncs = T_BANKS[k]
            if rows_of(c0 + ncs - 1) == P:
                return act.activation(pt_hi[:, c0:c0 + ncs, :], banks[:, bank, 0:ncs * P].rearrange("p (c n) -> p c n", n=P), ACT.Copy)
            r = rows_of(c0 + ncs - 1)
            act.activation(pt_hi[:, c0:c0 + ncs - 1, :],
                           banks[:, bank, 0:(ncs - 1) * P].rearrange("p (c n) -> p c n", n=P), ACT.Copy)
            return act.activation(pt_hi[0:r, c0 + ncs - 1, :], banks[0:r, bank, (ncs - 1) * P:ncs * P], ACT.Copy)

        def rest_of_probs(dve, k, bank):
            c0, ncs = T_BANKS[k]
            full = ncs if rows_of(c0 + ncs - 1) == P else ncs - 1
            at = slice(c0, c0 + full)
            ins = dve.tensor_tensor(pt_lo[:, at, :], banks[:, bank, 0:full * P].rearrange("p (c n) -> p c n", n=P),
                                    pt_hi[:, at, :].bitcast(F32), ALU.subtract)
            if full < ncs:
                c, r = c0 + full, rows_of(c0 + full)
                ins = dve.tensor_tensor(pt_lo[0:r, c, :], banks[0:r, bank, full * P:ncs * P],
                                        pt_hi[0:r, c, :].bitcast(F32), ALU.subtract)
            return ins

        def group_tables_act(act, rnd):
            act.dma_start(wst[0][:, 0:2, :].rearrange("p a n -> p (a n)").rearrange("p (t n) -> p t n", t=XT),
                          of_round(g_wk, rnd)).then_inc(gw_in, 16)
            act.dma_start(wst[0][:, 2:4, :].rearrange("p a n -> p (a n)").rearrange("p (t n) -> p t n", t=XT),
                          of_round(g_wv, rnd)).then_inc(gw_in, 16)
            act.dma_start(wst[0][:, 4:8, :], of_round(g_wq, rnd)).then_inc(gw_in, 16)
            act.dma_start(wst[1][:, 0:4, :], of_round(g_wo, rnd)).then_inc(gw_in, 16)
            act.dma_start(norm_sb[:, :], g_norm[bass.ds(rnd, 1)].rearrange("r p n -> p (r n)")).then_inc(gw_in, 16)
            act.dma_start(select[:, :], select_c).then_inc(gw_in, 16)
            act.dma_start(spread[:, :], spread_c).then_inc(gw_in, 16)
            act.wait_ge(gw_in, 112 * rnd + 112)
            act.activation(go_hi[:, :, :], wst[1][:, 0:4, :], ACT.Copy).then_inc(g_hi, 1)
            for g in range(KV_HEADS):
                act.wait_ge(g_raw, 7 * rnd + g + 1)
                act.activation(gk_hi[:, g, :, :], gk_raw[:, :, :], ACT.Copy).then_inc(g_hi, 1)
            act.wait_ge(g_raw, 7 * rnd + 5)
            act.activation(gq_hi[:, :, :], gq_raw[:, :, :], ACT.Copy).then_inc(g_hi, 1)
            for b in range(BATCH):
                act.wait_ge(g_raw, 7 * rnd + 6 + b)
                act.activation(gv_hi[:, b, :, :], gv_raw[:, :, :], ACT.Copy).then_inc(g_hi, 1)

        def group_tiles_act(act, g0, a0):
            def step(i, u):
                g = g0 + i
                if there(i, -2):
                    if there(i, -3):
                        act.wait_ge(g_o, g - 2)
                    for k, bank in ((0, 3), (1, 4)):
                        act.wait_ge(g_pt_raw, 3 * g - 5 + k)
                        copy_probs(act, k, bank).then_inc(g_pt_hi, 1)
                if there(i, 2):
                    act.wait_ge(xs_ready, a0 + i + 3)
                    if there(i, 1):
                        act.wait_ge(g_rms, g + 2)
                    act.activation(squares[:, :], xs[:, u % 2, :], ACT.Square, accum_out=ssq).then_inc(g_sq, 1)
                if there(i, 1):
                    act.wait_ge(g_xt_raw, g + 2)
                    if there(i, 0):
                        act.wait_ge(g_q, g + 1)
                    act.activation(xt_hi[:, 0, :, :].rearrange("p t n -> p (t n)"), banks[:, 5, :], ACT.Copy).then_inc(g_xt_hi, 1)
                if there(i, -2):
                    act.wait_ge(g_pt_raw, 3 * g - 3)
                    copy_probs(act, 2, 3).then_inc(g_pt_hi, 1)
                if there(i, -1):
                    act.wait_ge(g_shifted, 3 * g)
                    pr = probs[:, (u - 1) % 2, :]
                    act.activation(pr, pr, ACT.Exp, scale=GROUP_SCALE).then_inc(g_exp, 1)
                if there(i, 1):
                    act.wait_ge(g_q, g + 2)
                    if there(i, 0):
                        act.wait_ge(g_qt_raw, g + 1)
                    act.activation(q_sb[:, :], banks[:, 7, :], ACT.Copy).then_inc(g_q_sb, 1)
                if there(i, 2):
                    act.wait_ge(g_rms, g + 3)
                    if there(i, 1):
                        act.wait_ge(g_xt_raw, g + 2)
                    act.activation(xn[:, :], xs[:, u % 2, :], ACT.Copy, scale=rms).then_inc(g_xn, 1)
                if there(i, 1):
                    act.wait_ge(g_qt_raw, g + 2)
                    if there(i, -1):
                        act.wait_ge(g_scores, 3 * g)
                    act.activation(qt_hi[:, (u + 1) % 2, :, :].rearrange("p t n -> p (t n)"), banks[:, 5, :],
                                   ACT.Copy).then_inc(g_qt_hi, 1)
                if there(i, -2):
                    act.wait_ge(g_ot_raw, g - 1)
                    if there(i, -3):
                        act.wait_ge(g_out, g - 2)
                    act.activation(ot_hi[:, :, :].rearrange("p t n -> p (t n)"), banks[:, 5, :], ACT.Copy).then_inc(g_ot_hi, 1)

            sweep(act, -2, TILES + 1, step)

        BIAS_LINKS = 20

        def bias_dve(dve, rnd):
            links = 0

            def linked(ins):
                nonlocal links
                links += 1
                ins.then_inc(bias_link, 1)
                dve.wait_ge(bias_link, BIAS_LINKS * rnd + links)

            dve.wait_ge(aux_in, 80 * rnd + 80)
            linked(dve.tensor_copy(idx_f[:, 0:4], idx_i[:, :]))
            linked(dve.tensor_scalar(idx_f[:, 4:8], idx_f[:, 0:4], float(TOK), None, ALU.add))
            for n in range(8):
                linked(dve.tensor_scalar(hot[:, n, :], tok_sb[:, :], idx_f[:, n:n + 1], None, ALU.is_equal))
            for n, m in ((0, 1), (0, 4), (0, 5), (2, 3), (2, 6), (2, 7)):
                linked(dve.tensor_tensor(hot[:, n, :], hot[:, n, :], hot[:, m, :], ALU.max))
            linked(dve.tensor_tensor(hot[:, 0, :], hot[:, 0, :], hot[:, 2, :], ALU.is_gt))
            linked(dve.tensor_scalar(m_sb[:, :, :], m_sb[:, :, :], -1.0, 1.0, ALU.mult, ALU.add))

            def outer(dst, s, n):
                mask = m_sb[:, s, :].unsqueeze(2).broadcast_to([P, TILES, TOK])
                token = hot[:, n, :].unsqueeze(1).broadcast_to([P, TILES, TOK])
                return dve.tensor_tensor(dst[:, :, :], mask, token, ALU.mult)

            outer(bias8, 0, 0)
            linked(outer(bias_b, 1, 2))
            linked(dve.tensor_tensor(bias8[:, :, :], bias8[:, :, :], bias_b[:, :, :], ALU.add))
            assert links == BIAS_LINKS
            dve.tensor_scalar(bias8[:, :, :], bias8[:, :, :], -SUPPRESS / DENSE_SCALE, None, ALU.mult)

        def dense_tables_dve(dve, rnd, b):
            mask = half[:, :].unsqueeze(2).broadcast_to([P, 2, TOK])
            own = bass.ds(b * TOK, TOK)
            dve.tensor_tensor(k_bd[:, :, :].rearrange("p q (h k) -> p q h k", k=TOK),
                              k_t[:, :, own].unsqueeze(2).broadcast_to([P, PAIRS, 2, TOK]),
                              half[:, :].unsqueeze(1).unsqueeze(3).broadcast_to([P, PAIRS, 2, TOK]),
                              ALU.mult).then_inc(bd_ready, 1)
            dve.wait_ge(zero_done, rnd * BATCH + b + 1)
            for p in range(PAIRS):
                at = 2 * TOK * p - window_start(p)
                dve.tensor_tensor(v_bd[:, p, at:at + 2 * TOK].rearrange("p (h k) -> p h k", k=TOK),
                                  v_t[:, p, own].unsqueeze(1).broadcast_to([P, 2, TOK]), mask, ALU.mult).then_inc(bd_ready, 1)
            base = (rnd * BATCH + b) * GROUPS
            for n in range(CT * len(S_BANKS)):
                ct, (h0, nh) = n // len(S_BANKS), S_BANKS[n % len(S_BANKS)]
                cols = slice(h0 * TOK, (h0 + nh) * TOK)
                dve.wait_ge(tab_hi, base + n + 1)
                dve.tensor_tensor(kt_lo[:, ct, cols], banks[:, n % 8, 0:nh * TOK], kt_hi[:, ct, cols].bitcast(F32),
                                  ALU.subtract).then_inc(tab_lo, 1)
            for c in range(CHUNKS):
                n, r = CT * len(S_BANKS) + c, rows_of(c)
                dve.wait_ge(tab_hi, base + n + 1)
                dve.tensor_tensor(vt_lo[0:r, c, :], banks[0:r, n % 8, :], vt_hi[0:r, c, :].bitcast(F32),
                                  ALU.subtract).then_inc(tab_lo, 1)

        def slot(i):
            return x_ring[:, i, :] if isinstance(i, int) else x_ring[:, bass.ds(i, 1), :].rearrange("p a n -> p (a n)")

        def heads3(ap, nh):
            return ap.rearrange("p (h k) -> p h k", h=nh)

        def dense_tiles_dve(dve, g0, a0):
            def xt_rest(i, u):
                dve.wait_ge(d_xt_hi, g0 + i + 1)
                dve.tensor_tensor(xt_lo[:, u % 2, :, :].rearrange("p t n -> p (t n)"), banks[:, 6, :],
                                  xt_hi[:, u % 2, :, :].rearrange("p t n -> p (t n)").bitcast(F32), ALU.subtract).then_inc(d_xt_lo, 1)

            def step(i, u):
                g = g0 + i
                pr = probs[:, u % 2, :]
                if there(i, -3):
                    dve.wait_ge(d_out, g - 2)
                    dve.wait_ge(d_bo_added, g - 2)
                    dve.tensor_tensor(slot(i - 3), banks[:, 7, :], slot(i - 3), ALU.add).then_inc(x_updated, 1)
                if there(i, -2):
                    for k in range(3):
                        dve.wait_ge(d_pt_hi, 3 * g - 5 + k)
                        rest_of_probs(dve, k, 3 + k).then_inc(d_pt_lo, 1)
                if isinstance(i, int) and i == 0:
                    xt_rest(0, 0)
                if there(i, 0):
                    bias = bias8[:, i, :] if isinstance(i, int) else bias8[:, bass.ds(i, 1), :].rearrange("p a n -> p (a n)")
                    for k, (h0, nh) in enumerate(S_BANKS):
                        dve.wait_ge(d_scores, 3 * g + k + 1)
                        dve.tensor_tensor(heads3(pr[:, h0 * TOK:(h0 + nh) * TOK], nh), heads3(banks[:, k, 0:nh * TOK], nh),
                                          bias.unsqueeze(1).broadcast_to([P, nh, TOK]), ALU.add).then_inc(d_biased, 1)
                if there(i, 1, 1):
                    xt_rest(i + 1, u + 1)
                if there(i, 0):
                    wide = heads3(pr, HEADS)
                    dve.wait_ge(d_biased, 3 * g + 3)
                    dve.tensor_reduce(row_max, wide, X, ALU.max).then_inc(d_max, 1)
                    dve.wait_ge(d_max, g + 1)
                    dve.tensor_tensor(wide, wide, row_max.unsqueeze(2).broadcast_to([P, HEADS, TOK]),
                                      ALU.subtract).then_inc(d_shifted, 1)
                    dve.wait_ge(d_exp, g + 1)
                    dve.tensor_reduce(row_sum, wide, X, ALU.add).then_inc(d_sum, 1)
                    dve.wait_ge(d_sum, g + 1)
                    dve.reciprocal(row_rcp, row_sum).then_inc(d_rcp, 1)
                    dve.wait_ge(d_rcp, g + 1)
                    dve.tensor_tensor(wide, wide, row_rcp.unsqueeze(2).broadcast_to([P, HEADS, TOK]),
                                      ALU.mult).then_inc(d_probs, 1)

            sweep(dve, 0, TILES + 2, step)

        def group_tables_dve(dve, rnd):
            dve.wait_ge(g_proj, 3 * rnd + 1)
            dve.tensor_copy(k1[:, :], banks[:, 0, 0:BATCH * TOK]).then_inc(g_built, 1)
            for b in range(BATCH):
                dve.wait_ge(g_proj, 3 * rnd + b + 2)
                dve.tensor_copy(v1[0:TOK, b, :], banks[0:TOK, 4 + b, 0:P]).then_inc(g_built, 1)
            for g in range(KV_HEADS):
                dve.wait_ge(g_spread, KV_HEADS * rnd + g + 1)
                if g >= 1:
                    dve.wait_ge(g_lo, 6 * rnd + g)
                dve.tensor_tensor(gk_raw[:, :, :].rearrange("p b (r k) -> p b r k", k=TOK),
                                  banks[:, g, 0:BATCH * TOK].rearrange("p (b k) -> p b k", k=TOK).unsqueeze(2)
                                  .broadcast_to([P, BATCH, 4, TOK]),
                                  quarter[:, :].unsqueeze(1).unsqueeze(3).broadcast_to([P, BATCH, 4, TOK]),
                                  ALU.mult).then_inc(g_raw, 1)
                dve.wait_ge(g_hi, 8 * rnd + g + 2)
                dve.tensor_tensor(gk_lo[:, g, :, :], gk_raw[:, :, :], gk_hi[:, g, :, :].bitcast(F32), ALU.subtract).then_inc(g_lo, 1)
            dve.wait_ge(gw_in, 112 * rnd + 112)
            for ct in range(CT):
                ins = dve.tensor_scalar(gq_raw[:, ct, :], wst[0][:, 4 + ct, :], norm_sb[:, ct:ct + 1], None, ALU.mult)
            ins.then_inc(g_raw, 1)
            dve.tensor_tensor(go_lo[:, :, :], wst[1][:, 0:4, :], go_hi[:, :, :].bitcast(F32), ALU.subtract)
            dve.wait_ge(g_hi, 8 * rnd + 6)
            dve.tensor_tensor(gq_lo[:, :, :], gq_raw[:, :, :], gq_hi[:, :, :].bitcast(F32), ALU.subtract)
            for b in range(BATCH):
                if b >= 1:
                    dve.wait_ge(g_lo, 6 * rnd + KV_HEADS + b)
                dve.memset(gv_raw[:, :, :], 0.0).then_inc(g_cleared, 1)
                dve.wait_ge(g_cleared, 2 * rnd + b + 1)
                dve.tensor_copy(gv_raw[:, :, GROUP_D], member[:, :])
                for c in range(CHUNKS):
                    r = rows_of(c)
                    n = b * CHUNKS + c
                    dve.wait_ge(g_rep, BATCH * CHUNKS * rnd + n + 1)
                    for m, h in enumerate(heads_of(c)):
                        s0, grp = SLOT[c] + m, h // 4
                        ins = dve.tensor_scalar(gv_raw[0:r, s0, 0:GROUP_D], banks[0:r, 6 + n % 2, grp * GROUP_D:(grp + 1) * GROUP_D],
                                                member[0:r, s0:s0 + 1], None, ALU.mult)
                    ins.then_inc(g_rep_read, 1)
                dve.wait_ge(g_rep_read, BATCH * CHUNKS * rnd + (b + 1) * CHUNKS)
                dve.sem_inc(g_raw, 1)
                dve.wait_ge(g_hi, 8 * rnd + 7 + b)
                dve.tensor_tensor(gv_lo[:, b, :, :], gv_raw[:, :, :], gv_hi[:, b, :, :].bitcast(F32), ALU.subtract).then_inc(g_lo, 1)

        def group_tiles_dve(dve, g0, a0):
            def step(i, u):
                g = g0 + i

                def part(k):
                    h0, nh = S_BANKS[k]
                    scores = heads3(banks[:, k, 0:nh * TOK], nh)
                    dve.wait_ge(g_scores, 3 * g + k + 1)
                    dve.tensor_reduce(row_max[:, h0:h0 + nh], scores, X, ALU.max).then_inc(g_max, 1)
                    dve.wait_ge(g_max, 3 * g + k + 1)
                    dve.tensor_tensor(heads3(probs[:, u % 2, h0 * TOK:(h0 + nh) * TOK], nh), scores,
                                      row_max[:, h0:h0 + nh].unsqueeze(2).broadcast_to([P, nh, TOK]),
                                      ALU.subtract).then_inc(g_shifted, 1)

                if there(i, -2):
                    for k, bank in ((0, 3), (1, 4)):
                        dve.wait_ge(g_pt_hi, 3 * g - 5 + k)
                        rest_of_probs(dve, k, bank).then_inc(g_pt_lo, 1)
                if there(i, 1):
                    dve.wait_ge(g_xt_hi, g + 2)
                    dve.tensor_tensor(xt_lo[:, 0, :, :].rearrange("p t n -> p (t n)"), banks[:, 5, :],
                                      xt_hi[:, 0, :, :].rearrange("p t n -> p (t n)").bitcast(F32), ALU.subtract).then_inc(g_xt_lo, 1)
                if there(i, -2):
                    dve.wait_ge(g_pt_hi, 3 * g - 3)
                    rest_of_probs(dve, 2, 3).then_inc(g_pt_lo, 1)
                if there(i, -3):
                    dve.wait_ge(g_out, g - 2)
                    dve.tensor_tensor(slot(i - 3), banks[:, 6, :], slot(i - 3), ALU.add).then_inc(x_updated, 1)
                if there(i, 0):
                    part(0)
                    part(1)
                if there(i, -2):
                    dve.wait_ge(g_o, g - 1)
                    if there(i, -3):
                        dve.wait_ge(g_ot_raw, g - 2)
                    per_side = HEADS // 2
                    for side in range(2):
                        o = banks[:, 6 + side, 0:per_side * GV].rearrange("p (h n) -> p h n", n=GV)
                        dve.reciprocal(row_rcp[:, side * per_side:(side + 1) * per_side], o[:, :, GROUP_D]).then_inc(g_rcp, 1)
                    for side in range(2):
                        o = banks[:, 6 + side, 0:per_side * GV].rearrange("p (h n) -> p h n", n=GV)
                        dve.wait_ge(g_rcp, 2 * g - 3 + side)
                        dve.tensor_tensor(o_sb[:, side * C // 2:(side + 1) * C // 2].rearrange("p (h n) -> p h n", n=GROUP_D),
                                          o[:, :, 0:GROUP_D],
                                          row_rcp[:, side * per_side:(side + 1) * per_side].unsqueeze(2)
                                          .broadcast_to([P, per_side, GROUP_D]), ALU.mult).then_inc(g_o_sb, 1)
                if there(i, 1):
                    dve.wait_ge(g_qt_hi, g + 2)
                    dve.tensor_tensor(qt_lo[:, (u + 1) % 2, :, :].rearrange("p t n -> p (t n)"), banks[:, 5, :],
                                      qt_hi[:, (u + 1) % 2, :, :].rearrange("p t n -> p (t n)").bitcast(F32), ALU.subtract).then_inc(g_qt_lo, 1)
                if there(i, 0):
                    part(2)
                if there(i, -2):
                    dve.wait_ge(g_ot_hi, g - 1)
                    dve.tensor_tensor(ot_lo[:, :, :].rearrange("p t n -> p (t n)"), banks[:, 5, :],
                                      ot_hi[:, :, :].rearrange("p t n -> p (t n)").bitcast(F32), ALU.subtract).then_inc(g_ot_lo, 1)

            sweep(dve, -2, TILES + 2, step)


        def inverse_rms(pool, g, i):
            pool.wait_ge(g_sq, g + i + 1)
            if i >= 1:
                pool.wait_ge(g_xn, g + i)
            pool.sem_inc(passed, 1)
            pool.tensor_scalar(mean_sq, ssq, 1.0 / C, EPS, ALU.mult, ALU.add).then_inc(g_var, 1)
            pool.wait_ge(g_var, g + i + 1)
            pool.tensor_tensor(rms, mean_sq, exponent, ALU.pow).then_inc(g_rms, 1)

        block = ctx.enter_context(nc.Block())

        @block.tensor
        def _(pe):
            pe.wait_ge(const_in, 16 * 5)
            with pe.Fori(0, ROUNDS) as rnd:
                for n in range(4):
                    pe.wait_ge(w_in[n % 2], 48 * rnd + 16 * (n // 2 + 1))
                    for m in range(4):
                        t = 4 * n + m
                        if t >= 8:
                            pe.wait_ge(proj_read, 16 * rnd + t - 7)
                        for kt in range(XT):
                            mm = pe.matmul(banks[:, t % 8, 0:BATCH * TOK], wst[n % 2][:, kt, m * P:(m + 1) * P],
                                           ctx_sb[:, kt, :], start=kt == 0, stop=kt == XT - 1)
                        mm.then_inc(proj_done, 1)
                stage_end(pe, rnd, 0)
                with pe.Fori(0, BATCH) as b:
                    dense_tables_pe(pe, rnd, b)
                    stage_end(pe, rnd, 2 * b + 1)
                    dense_tiles_pe(pe, (rnd * BATCH + b) * TILES, (rnd * 2 * BATCH + b) * TILES)
                    stage_end(pe, rnd, 2 * b + 2)
                group_tables_pe(pe, rnd)
                stage_end(pe, rnd, 5)
                with pe.Fori(0, BATCH) as b:
                    group_tiles_pe(pe, b, (rnd * BATCH + b) * TILES, (rnd * 2 * BATCH + b + BATCH) * TILES)
                    stage_end(pe, rnd, b + 6)

        @block.scalar
        def _(act):
            with act.Fori(0, ROUNDS) as rnd:
                dense_project_act(act, rnd)
                stage_end(act, rnd, 0)
                with act.Fori(0, BATCH) as b:
                    base = (rnd * BATCH + b) * GROUPS
                    for n in range(CT * len(S_BANKS)):
                        ct, (h0, nh) = n // len(S_BANKS), S_BANKS[n % len(S_BANKS)]
                        act.wait_ge(tab_done, base + n + 1)
                        act.activation(kt_hi[:, ct, h0 * TOK:(h0 + nh) * TOK], banks[:, n % 8, 0:nh * TOK],
                                       ACT.Copy).then_inc(tab_hi, 1)
                    for c in range(CHUNKS):
                        n, r = CT * len(S_BANKS) + c, rows_of(c)
                        act.wait_ge(tab_done, base + n + 1)
                        act.activation(vt_hi[0:r, c, :], banks[0:r, n % 8, :], ACT.Copy).then_inc(tab_hi, 1)
                    stage_end(act, rnd, 2 * b + 1)
                    dense_tiles_act(act, (rnd * BATCH + b) * TILES)
                    stage_end(act, rnd, 2 * b + 2)
                group_tables_act(act, rnd)
                stage_end(act, rnd, 5)
                with act.Fori(0, BATCH) as b:
                    group_tiles_act(act, (rnd * BATCH + b) * TILES, (rnd * 2 * BATCH + b + BATCH) * TILES)
                    stage_end(act, rnd, b + 6)

        @block.vector
        def _(dve):
            dve.wait_ge(const_in, 16 * 5)
            with dve.Fori(0, ROUNDS) as rnd:
                bias_dve(dve, rnd)
                stage_end(dve, rnd, 0)
                with dve.Fori(0, BATCH) as b:
                    dense_tables_dve(dve, rnd, b)
                    stage_end(dve, rnd, 2 * b + 1)
                    dense_tiles_dve(dve, (rnd * BATCH + b) * TILES, (rnd * 2 * BATCH + b) * TILES)
                    stage_end(dve, rnd, 2 * b + 2)
                group_tables_dve(dve, rnd)
                stage_end(dve, rnd, 5)
                with dve.Fori(0, BATCH) as b:
                    group_tiles_dve(dve, (rnd * BATCH + b) * TILES, (rnd * 2 * BATCH + b + BATCH) * TILES)
                    stage_end(dve, rnd, b + 6)

        @block.gpsimd
        def _(pool):
            pool.memset(exponent, -0.5).then_inc(exponent_set, 1)
            pool.wait_ge(exponent_set, 1)
            with pool.Fori(0, ROUNDS) as rnd:
                stage_end(pool, rnd, 0)
                with pool.Fori(0, BATCH) as b:
                    pool.memset(v_bd[:, :, :], 0.0).then_inc(zero_done, 1)
                    stage_end(pool, rnd, 2 * b + 1)
                    stage, g = rnd * 2 * BATCH + b, (rnd * BATCH + b) * TILES
                    for i in range(TILES):
                        pool.wait_ge(x_in[i], 16 * stage + 16)
                        if i >= 2:
                            pool.wait_ge(d_xt_raw, g + i - 1)
                        pool.sem_inc(passed, 1)
                        pool.tensor_copy(xs[:, i % 2, :], x_ring[:, i, :]).then_inc(xs_ready, 1)
                        pool.tensor_tensor(x_ring[:, i, :], x_ring[:, i, :], bo_sb[:, :], ALU.add).then_inc(d_bo_added, 1)
                    stage_end(pool, rnd, 2 * b + 2)
                stage_end(pool, rnd, 5)
                with pool.Fori(0, BATCH) as b:
                    stage, g = rnd * 2 * BATCH + b + BATCH, (rnd * BATCH + b) * TILES
                    for i in range(TILES):
                        pool.wait_ge(x_in[i], 16 * stage + 16)
                        if i >= 2:
                            pool.wait_ge(g_xn, g + i - 1)
                        pool.sem_inc(passed, 1)
                        pool.tensor_copy(xs[:, i % 2, :], x_ring[:, i, :]).then_inc(xs_ready, 1)
                        if i >= 1:
                            inverse_rms(pool, g, i - 1)
                    inverse_rms(pool, g, TILES - 1)
                    stage_end(pool, rnd, b + 6)

        @block.sync
        def _(sp):
            for dst, src in ((ident, ident_c), (half, half_c), (quarter, quarter_c), (member, member_c)):
                sp.dma_start(dst[:, :], src).then_inc(const_in, 16)
            sp.dma_start(ctx_sb[:, :, :], ctx_t.rearrange("(t p) n -> p t n", p=P)).then_inc(const_in, 16)
            x_t = x.rearrange("b (t p) n -> b t p n", p=P)
            out_t = out.rearrange("b (t p) n -> b t p n", p=P)
            for i in range(TILES):
                sp.dma_start(x_ring[:, i, :], x_t[0, i]).then_inc(x_in[i], 16)

            def stage(s, dst, src, src_ready=None):
                def load(i):
                    sp.wait_ge(x_out[i], 16 * s + 16)
                    sp.dma_start(x_ring[:, i, :], src[i]).then_inc(x_in[i], 16)

                for i in range(TILES):
                    sp.wait_ge(x_updated, TILES * s + i + 1)
                    sp.dma_start(dst[i], x_ring[:, i, :]).then_inc(x_out[i], 16)
                    if src is not None and i >= 1:
                        load(i - 1)
                if src is not None:
                    load(TILES - 1)

            stage(0, x_mid[0], x_t[1])
            stage(1, x_mid[1], x_mid[0])
            with sp.Fori(1, ROUNDS * 2 - 1) as t:
                stage(2 * t, x_mid[0], x_mid[1])
                stage(2 * t + 1, x_mid[1], x_mid[0])
            stage(ROUNDS * 4 - 2, out_t[0], x_mid[1])
            stage(ROUNDS * 4 - 1, out_t[1], None)
            for i in range(TILES):
                sp.wait_ge(x_out[i], 16 * ROUNDS * 4)


def constants():
    rows = np.arange(P)
    keys = np.arange(KEYS)
    member = np.zeros((P, SLOTS), np.float32)
    for c in range(CHUNKS):
        for m, h in enumerate(heads_of(c)):
            member[:, SLOT[c] + m] = (c * P + rows) // TOK == h
    return {
        "ident_c": np.eye(P, dtype=np.float32),
        "half_c": (rows[:, None] // DENSE_D == np.arange(2)).astype(np.float32),
        "quarter_c": (rows[:, None] // GROUP_D == np.arange(4)).astype(np.float32),
        "member_c": member,
        "select_c": (keys[None, :] % TOK == np.arange(TOK)[:, None]).astype(np.float32),
        "spread_c": np.concatenate([(rows[:, None] == g * GROUP_D + rows[None, :] % GROUP_D).astype(np.float32)
                                    for g in range(KV_HEADS)], axis=1),
        "token_c": np.ascontiguousarray(np.broadcast_to(np.arange(TOK, dtype=np.float32), (P, TOK))),
    }


def kernel(**inputs):
    import concourse.bacc as bacc
    from concourse.bass_utils import run_bass_kernel_spmd as run

    a = {k: np.asarray(v) for k, v in inputs.items()}

    def both(name):
        return np.stack([a[f"L{n}_xattn_{name}"] for n in (0, 2)])

    def both_g(name):
        return np.stack([a[f"L{n}_xattn_{name}"] for n in (1, 3)])

    def on_rows(v):
        return np.broadcast_to(v[:, None, :], (v.shape[0], P, v.shape[1]))

    arrays = {
        "x": a["x"],
        "ctx_t": a["ctx_2048"].reshape(BATCH * TOK, CTX).T,
        "mask_a": a["mask_S_fk1"].reshape(TILES, P).T,
        "mask_b": a["mask_S_fk0"].reshape(TILES, P).T,
        "d_wq_t": both("Wq").transpose(0, 2, 1),
        "d_wk": both("Wk"),
        "d_wv": both("Wv"),
        "d_wo": both("Wo"),
        "d_bo": on_rows(both("bo")),
        "d_idx": on_rows(np.concatenate([both("token_indices_A"), both("token_indices_B")], axis=1)),
        "g_wq": both_g("wq"),
        "g_wk": both_g("wk"),
        "g_wv": both_g("wv"),
        "g_wo": both_g("wo"),
        "g_norm": both_g("norm_w").reshape(ROUNDS, CT, P).transpose(0, 2, 1),
        **constants(),
    }
    arrays = {k: np.ascontiguousarray(v) for k, v in arrays.items()}
    nc = bacc.Bacc("TRN2", target_bir_lowering=False, num_devices=1)
    args = [nc.dram_tensor(k, v.shape, mybir.dt.from_np(v.dtype), kind="ExternalInput").ap() for k, v in arrays.items()]
    out = nc.dram_tensor("out", (BATCH, ROWS, C), F32, kind="ExternalOutput").ap()
    build(nc, *args, out)
    r = run(nc, [arrays], core_ids=[0])
    return r.results[0]["out"]
```

```python
from contextlib import ExitStack

import numpy as np
import concourse.bass as bass
from concourse import mybir

ALU = mybir.AluOpType
ACT = mybir.ActivationFunctionType
X = mybir.AxisListType.X
F32 = mybir.dt.float32
F32R = mybir.dt.float32r
I32 = mybir.dt.int32

P = 128
ROUNDS = 2
BATCH, ROWS, C = 2, 2048, 512
TOK, CTX = 77, 1024
HEADS = 16
DENSE_D, GROUP_D, KV_HEADS = 64, 32, 4
INNER = HEADS * DENSE_D
KEYS = HEADS * TOK
TILES = ROWS // P
CT, XT = C // P, CTX // P
PAIRS = INNER // P
CHUNKS = -(-KEYS // P)
BANK = 512
DUOS = TILES // 2
UNROLL = 2
TILE_LOOP = (3, TILES - 3)
DUO_LOOP = (1, DUOS - 3)
EPS = 1e-5
SUPPRESS = 20.0
DENSE_SCALE = DENSE_D ** -0.5
GROUP_SCALE = float(np.float32(1.0) / np.sqrt(GROUP_D).astype(np.float32))

S_BANKS = [(0, 6), (6, 6), (12, 4)]
T_BANKS = [(0, 4), (4, 4), (8, 2)]


def rows_of(c):
    return min(P, KEYS - c * P)


def pairs_of(c):
    return range(c * P // (2 * TOK), (c * P + rows_of(c) - 1) // (2 * TOK) + 1)


GROUP_CHUNKS = [range(g * 4 * TOK // P, ((g + 1) * 4 * TOK - 1) // P + 1) for g in range(KV_HEADS)]
FIRST_SLOT = [sum(len(x) for x in GROUP_CHUNKS[:g]) for g in range(KV_HEADS + 1)]
SLOTS = FIRST_SLOT[KV_HEADS]
WINDOW = 3 * P


def window_start(p):
    return p * 2 * TOK // P * P


def build(nc, x, ctx_t, mask_a, mask_b, d_wq_t, d_wk, d_wv, d_wo, d_bo, d_idx,
          g_wq, g_wk, g_wv, g_wo, g_norm, ident_c, half_c, quarter_c, member_c, select_c, spread_c, token_c, out):
    ctx = ExitStack()
    with ctx:
        def sem(name):
            return ctx.enter_context(nc.semaphore(name))

        def sb(name, shape, dt=F32, scope=ctx):
            return scope.enter_context(nc.sbuf_tensor(name, shape, dt))

        ident = sb("ident", [P, P])
        half = sb("half", [P, 2])
        quarter = sb("quarter", [P, 4])
        member = sb("member", [P, SLOTS, 4])
        ctx_sb = sb("ctx_sb", [P, XT, BATCH * TOK])
        x_ring = sb("x_ring", [P, TILES, C])
        wst = [sb("wst0", [P, XT, C])]
        with ExitStack() as s:
            wst.append(sb("wst1", [P, XT, C], F32, s))
        with ExitStack() as s:
            qt_hi = sb("qt_hi", [P, 2, CT, 2 * P], F32R, s)
            qt_lo = sb("qt_lo", [P, 2, CT, 2 * P], F32R, s)
        sb("wst1_place", [P, XT, C])
        small = sb("small", [P, 88])
        banks = ctx.enter_context(nc.psum_tensor("banks", [P, 8, BANK], F32))

        with ExitStack() as s:
            kt_hi = sb("kt_hi", [P, CT, KEYS], F32R, s)
            kt_lo = sb("kt_lo", [P, CT, KEYS], F32R, s)
            vt_hi = sb("vt_hi", [P, CHUNKS, C], F32R, s)
            vt_lo = sb("vt_lo", [P, CHUNKS, C], F32R, s)
        with ExitStack() as s:
            gq_hi = sb("gq_hi", [P, CT, C], F32R, s)
            gq_lo = sb("gq_lo", [P, CT, C], F32R, s)
            go_hi = sb("go_hi", [P, CT, C], F32R, s)
            go_lo = sb("go_lo", [P, CT, C], F32R, s)
            gk_hi = sb("gk_hi", [P, KV_HEADS, BATCH, 4 * TOK], F32R, s)
            gk_lo = sb("gk_lo", [P, KV_HEADS, BATCH, 4 * TOK], F32R, s)
            gv_hi = sb("gv_hi", [P, SLOTS, P], F32R, s)
            gv_lo = sb("gv_lo", [P, SLOTS, P], F32R, s)
            gv_raw = sb("gv_raw", [P, BATCH, SLOTS, P], F32, s)
        sb("tables_place", [P, 2 * CT * KEYS + 2 * CHUNKS * C])

        with ExitStack() as s:
            bias8 = sb("bias8", [P, TILES, TOK], F32, s)
            bo_sb = sb("bo_sb", [P, C], F32, s)
            k_t = sb("k_t", [P, PAIRS, BATCH * TOK], F32, s)
            v_t = sb("v_t", [P, PAIRS, BATCH * TOK], F32, s)
        with ExitStack() as s:
            ot_hi = sb("ot_hi", [P, CT, 2 * P], F32R, s)
            ot_lo = sb("ot_lo", [P, CT, 2 * P], F32R, s)
            g_pr = sb("g_pr", [P, 2, KEYS], F32, s)
            squares = sb("squares", [P, 2, C], mybir.dt.bfloat16, s)
        sb("layer_place", [P, 2 * CT * 2 * P + 2 * KEYS + C + 16])

        with ExitStack() as s:
            xt_hi = sb("xt_hi", [P, 2, CT, P], F32R, s)
            xt_lo = sb("xt_lo", [P, 2, CT, P], F32R, s)
            pt_hi = sb("pt_hi", [P, CHUNKS, P], F32R, s)
            pt_lo = sb("pt_lo", [P, CHUNKS, P], F32R, s)
            probs = sb("probs", [P, 2, KEYS], F32, s)
            xs = sb("xs", [P, 2, C], F32, s)
        with ExitStack() as s:
            k_bd = sb("k_bd", [P, PAIRS, 2 * TOK], F32, s)
            v_bd = sb("v_bd", [P, PAIRS, WINDOW], F32, s)
            tok_sb = sb("tok_sb", [P, TOK], F32, s)
            idx_i = sb("idx_i", [P, 4], I32, s)
            idx_f = sb("idx_f", [P, 8], F32, s)
            hot = sb("hot", [P, 8, TOK], F32, s)
            bias_b = sb("bias_b", [P, TILES, TOK], F32, s)
            m_sb = sb("m_sb", [P, 2, TILES], F32, s)
        with ExitStack() as s:
            gxt_hi = sb("gxt_hi", [P, CT, 2 * P], F32R, s)
            gxt_lo = sb("gxt_lo", [P, CT, 2 * P], F32R, s)
            gpt_hi = sb("gpt_hi", [P, CHUNKS, 2 * P], F32R, s)
            gpt_lo = sb("gpt_lo", [P, CHUNKS, 2 * P], F32R, s)
            xn = sb("xn", [P, 2, C], F32, s)
        with ExitStack() as s:
            gk_raw = sb("gk_raw", [P, BATCH, 4 * TOK], F32, s)
            gq_raw = sb("gq_raw", [P, CT, C], F32, s)
            k1 = sb("k1", [P, BATCH * TOK], F32, s)
            v1 = sb("v1", [P, BATCH, P], F32, s)
            spread = sb("spread", [P, KV_HEADS * P], F32, s)
            select = sb("select", [TOK, KEYS], F32, s)
            norm_sb = sb("norm_sb", [P, CT], F32, s)
        sb("work_place", [P, 2 * CT * 2 * P + 2 * CHUNKS * 2 * P + 2 * C + 16])

        row_max = small[:, 0:16]
        row_sum = small[:, 16:32]
        row_rcp = small[:, 32:48]
        g_sum = [small[:, 16:32], small[:, 0:16]]
        g_rcp_of = [small[:, 32:48], small[:, 56:72]]
        g_row_max = small[:, 72:88]
        ssq = small[:, 48:50]
        rms = small[:, 50:52]
        mean_sq = small[:, 52:54]
        exponent = small[:, 54:56]

        x_mid = nc.dram_tensor("x_mid", [BATCH, TILES, P, C], F32, kind="Internal").ap()

        const_in = sem("const_in")
        passed = sem("passed")
        stage_done = sem("stage_done")
        x_in = [sem(f"x_in{i}") for i in range(TILES)]
        x_out = [sem(f"x_out{i}") for i in range(TILES)]
        xs_ready = sem("xs_ready")
        x_updated = sem("x_updated")
        w_in = [sem("w_in0"), sem("w_in1")]
        gw_in = sem("gw_in")
        aux_in = sem("aux_in")
        proj_done, proj_read = sem("proj_done"), sem("proj_read")
        bd_ready, zero_done = sem("bd_ready"), sem("zero_done")
        tab_done, tab_hi, tab_lo = sem("tab_done"), sem("tab_hi"), sem("tab_lo")
        bias_link = sem("bias_link")
        d_xt_raw, d_xt_hi, d_xt_lo = sem("d_xt_raw"), sem("d_xt_hi"), sem("d_xt_lo")
        d_scores, d_biased, d_max = sem("d_scores"), sem("d_biased"), sem("d_max")
        d_shifted, d_exp, d_sum, d_rcp = sem("d_shifted"), sem("d_exp"), sem("d_sum"), sem("d_rcp")
        d_probs, d_bo_added = sem("d_probs"), sem("d_bo_added")
        d_pt_raw, d_pt_hi, d_pt_lo = sem("d_pt_raw"), sem("d_pt_hi"), sem("d_pt_lo")
        d_out = sem("d_out")
        g_proj, g_built, g_spread = sem("g_proj"), sem("g_built"), sem("g_spread")
        g_rep, g_rep_read = sem("g_rep"), sem("g_rep_read")
        g_raw, g_hi, g_lo = sem("g_raw"), sem("g_hi"), sem("g_lo")
        g_zero = sem("g_zero")
        exponent_set = sem("exponent_set")
        g_sq, g_var, g_rms, g_xn = sem("g_sq"), sem("g_var"), sem("g_rms"), sem("g_xn")
        g_xt_raw, g_xt_hi, g_xt_lo = sem("g_xt_raw"), sem("g_xt_hi"), sem("g_xt_lo")
        g_q, g_qt_hi, g_qt_lo = sem("g_q"), sem("g_qt_hi"), sem("g_qt_lo")
        g_scores, g_max, g_shifted, g_exp = sem("g_scores"), sem("g_max"), sem("g_shifted"), sem("g_exp")
        g_sum_done, g_rcp, g_probs = sem("g_sum_done"), sem("g_rcp"), sem("g_probs")
        g_pt_raw, g_pt_hi, g_pt_lo = sem("g_pt_raw"), sem("g_pt_hi"), sem("g_pt_lo")
        g_o, g_ot_hi, g_ot_lo = sem("g_o"), sem("g_ot_hi"), sem("g_ot_lo")
        g_v_hi, g_v_lo = sem("g_v_hi"), sem("g_v_lo")
        g_out = sem("g_out")

        STAGES = 8

        def stage_end(eng, rnd, n):
            eng.drain().then_inc(stage_done, 1)
            eng.wait_ge(stage_done, 4 * STAGES * rnd + 4 * (n + 1))
            eng.sem_inc(passed, 1)

        def sweep(eng, first, last, alike, step):
            for i in range(first, alike[0]):
                step(i, i)
            with eng.Fori(0, (alike[1] - alike[0]) // UNROLL) as j:
                for u in range(UNROLL):
                    step(UNROLL * j + (alike[0] + u), alike[0] + u)
            for i in range(alike[1], last + 1):
                step(i, i)

        def there(i, d, lo=0, n=TILES):
            return not isinstance(i, int) or lo <= i + d < n

        def duo(m, d):
            return there(m, d, 0, DUOS)

        def product(pe, dst, pairs, first=True, last=True, check=True):
            n = 3 * len(pairs)
            at = 0
            for (a_hi, a_lo), (b_hi, b_lo) in pairs:
                for a, b in ((a_hi, b_hi), (a_hi, b_lo), (a_lo, b_hi)):
                    mm = pe.matmul(dst, a, b, start=first and at == 0, stop=last and at == n - 1,
                                   skip_group_check=not check)
                    at += 1
            return mm

        GROUPS = CT * len(S_BANKS) + CHUNKS

        def dense_tables_pe(pe, rnd, b):
            base = (rnd * BATCH + b) * GROUPS
            pe.wait_ge(w_in[0], 48 * rnd + 48)
            pe.wait_ge(bd_ready, (rnd * BATCH + b) * 9 + 1)
            n = 0
            for ct in range(CT):
                for k, (h0, nh) in enumerate(S_BANKS):
                    if n >= 8:
                        pe.wait_ge(tab_lo, base + n - 7)
                    for p in range(h0 // 2, (h0 + nh) // 2):
                        at = (p - h0 // 2) * 2 * TOK
                        mm = pe.matmul(banks[:, n % 8, at:at + 2 * TOK], wst[0][:, p, ct * P:(ct + 1) * P],
                                       k_bd[:, p, :], start=True, stop=True)
                    mm.then_inc(tab_done, 1)
                    n += 1
            pe.wait_ge(w_in[1], 48 * rnd + 48)
            pe.wait_ge(bd_ready, (rnd * BATCH + b) * 9 + 9)
            for c in range(CHUNKS):
                pe.wait_ge(tab_lo, base + n - 7)
                for p in pairs_of(c):
                    at = c * P - window_start(p)
                    mm = pe.matmul(banks[0:rows_of(c), n % 8, :], v_bd[:, p, at:at + rows_of(c)], wst[1][:, p, :],
                                   start=p == pairs_of(c)[0], stop=p == pairs_of(c)[-1])
                mm.then_inc(tab_done, 1)
                n += 1

        def dense_tiles_pe(pe, g0, a0):
            def turn_x(i, u):
                pe.wait_ge(xs_ready, g0 + i + 1)
                for ct in range(CT):
                    mm = pe.transpose(banks[:, 6, ct * P:(ct + 1) * P], xs[:, u % 2, ct * P:(ct + 1) * P], ident[:, :])
                mm.then_inc(d_xt_raw, 1)

            def step(i, u):
                g = g0 + i
                if there(i, -2):
                    pe.wait_ge(d_probs, g - 1)
                    for k, (c0, ncs) in enumerate(T_BANKS):
                        if there(i, -3):
                            pe.wait_ge(d_pt_lo, 3 * g - 8 + k)
                        for c in range(c0, c0 + ncs):
                            mm = pe.transpose(banks[0:rows_of(c), 3 + k, (c - c0) * P:(c - c0 + 1) * P],
                                              probs[:, u % 2, c * P:c * P + rows_of(c)], ident[:, :])
                        mm.then_inc(d_pt_raw, 1)
                if isinstance(i, int) and i == 0:
                    turn_x(0, 0)
                if there(i, 0):
                    pe.wait_ge(d_xt_lo, g + 1)
                    for k, (h0, nh) in enumerate(S_BANKS):
                        if there(i, -1):
                            pe.wait_ge(d_biased, 3 * g - 2 + k)
                        cols = slice(h0 * TOK, (h0 + nh) * TOK)
                        product(pe, banks[:, k, 0:nh * TOK],
                                [((xt_hi[:, u % 2, ct, :], xt_lo[:, u % 2, ct, :]), (kt_hi[:, ct, cols], kt_lo[:, ct, cols]))
                                 for ct in range(CT)]).then_inc(d_scores, 1)
                if there(i, 1, 1):
                    turn_x(i + 1, u + 1)
                if there(i, -2):
                    if there(i, -3):
                        pe.wait_ge(x_updated, a0 + i - 2)
                    for c in range(CHUNKS):
                        if c % 4 == 0:
                            pe.wait_ge(d_pt_lo, 3 * g - 5 + c // 4)
                        r = rows_of(c)
                        mm = product(pe, banks[:, 7, :], [((pt_hi[0:r, c, :], pt_lo[0:r, c, :]), (vt_hi[0:r, c, :], vt_lo[0:r, c, :]))],
                                     first=c == 0, last=c == CHUNKS - 1)
                    mm.then_inc(d_out, 1)

            sweep(pe, 0, TILES + 1, TILE_LOOP, step)

        def group_tables_pe(pe, rnd):
            pe.wait_ge(gw_in, 112 * rnd + 112)
            wk = wst[0][:, 0:2, :].rearrange("p a n -> p (a n)").rearrange("p (t n) -> p t n", t=XT)
            wv = wst[0][:, 2:4, :].rearrange("p a n -> p (a n)").rearrange("p (t n) -> p t n", t=XT)
            for kt in range(XT):
                mm = pe.matmul(banks[:, 0, 0:BATCH * TOK], wk[:, kt, :], ctx_sb[:, kt, :], start=kt == 0, stop=kt == XT - 1)
            mm.then_inc(g_proj, 1)
            for b in range(BATCH):
                for kt in range(XT):
                    mm = pe.matmul(banks[0:TOK, 4 + b, 0:P], ctx_sb[:, kt, b * TOK:(b + 1) * TOK], wv[:, kt, :],
                                   start=kt == 0, stop=kt == XT - 1)
                mm.then_inc(g_proj, 1)
            pe.wait_ge(g_built, 3 * rnd + 1)
            for g in range(KV_HEADS):
                pe.matmul(banks[:, g, 0:BATCH * TOK], spread[:, g * P:(g + 1) * P], k1[:, :],
                          start=True, stop=True).then_inc(g_spread, 1)
            pe.wait_ge(g_built, 3 * rnd + 3)
            n = 0
            for b in range(BATCH):
                for c in range(CHUNKS):
                    if n >= 2:
                        pe.wait_ge(g_rep_read, BATCH * CHUNKS * rnd + n - 1)
                    r = rows_of(c)
                    pe.matmul(banks[0:r, 6 + n % 2, 0:P], select[:, c * P:c * P + r], v1[0:TOK, b, :],
                              start=True, stop=True).then_inc(g_rep, 1)
                    n += 1

        def group_tiles_pe(pe, b, visit, a0):
            d0 = visit * DUOS

            def scores(m, u, side):
                d = d0 + m
                for k, (h0, nh) in enumerate(S_BANKS):
                    if side == 0 and duo(m, -1):
                        pe.wait_ge(g_shifted, 6 * d - 2 + k)
                    if side == 1:
                        pe.wait_ge(g_shifted, 6 * d + 1 + k)
                    for grp in range(h0 // 4, -(-(h0 + nh) // 4)):
                        lo, hi = max(h0, 4 * grp), min(h0 + nh, 4 * grp + 4)
                        cols = slice((lo - 4 * grp) * TOK, (hi - 4 * grp) * TOK)
                        own = slice(side * P, (side + 1) * P)
                        mm = product(pe, banks[:, k, (lo - h0) * TOK:(hi - h0) * TOK],
                                     [((qt_hi[:, u % 2, grp, own], qt_lo[:, u % 2, grp, own]),
                                       (gk_hi[:, grp, b, cols], gk_lo[:, grp, b, cols]))])
                    mm.then_inc(g_scores, 1)

            def turn_probs(t, side, before):
                pe.wait_ge(g_probs, t + 1)
                for k, (c0, ncs) in enumerate(T_BANKS):
                    if before:
                        pe.wait_ge(g_pt_lo, 3 * t - 2 + k)
                    for c in range(c0, c0 + ncs):
                        mm = pe.transpose(banks[0:rows_of(c), 3 + k, (c - c0) * P:(c - c0 + 1) * P],
                                          g_pr[:, side, c * P:c * P + rows_of(c)], ident[:, :])
                    mm.then_inc(g_pt_raw, 1)

            def step(m, u):
                d = d0 + m
                if duo(m, 0):
                    pe.wait_ge(g_qt_lo, 2 * d + 2)
                    if duo(m, 1):
                        pe.wait_ge(g_xt_lo, 2 * d + 4)
                    scores(m, u, 0)
                if duo(m, -1):
                    turn_probs(2 * d - 1, 1, True)
                if duo(m, 1):
                    pe.wait_ge(g_xt_lo, 2 * d + 4)
                    for g in range(KV_HEADS):
                        if g % 2 == 0 and duo(m, -2):
                            pe.wait_ge(x_updated, a0 + 2 * m - 3 + g // 2)
                        mm = product(pe, banks[:, 6 + g // 2, g % 2 * 2 * P:(g % 2 + 1) * 2 * P],
                                     [((gq_hi[:, ct, g * P:(g + 1) * P], gq_lo[:, ct, g * P:(g + 1) * P]),
                                       (gxt_hi[:, ct, :], gxt_lo[:, ct, :])) for ct in range(CT)])
                        if g % 2:
                            mm.then_inc(g_q, 1)
                if duo(m, 0):
                    scores(m, u, 1)
                if duo(m, -1):
                    pe.wait_ge(g_v_lo, visit + 1)
                    pe.wait_ge(g_pt_lo, 6 * d)
                    for g in range(KV_HEADS):
                        if g % 2 == 0:
                            if duo(m, 1):
                                pe.wait_ge(g_qt_lo, 2 * d + 3 + g // 2)
                            elif duo(m, -2):
                                pe.wait_ge(x_updated, a0 + 2 * m - 3 + g // 2)
                        mm = product(pe, banks[:, 6 + g // 2, g % 2 * 2 * P:(g % 2 + 1) * 2 * P],
                                     [((gv_hi[0:rows_of(c), FIRST_SLOT[g] + n, :], gv_lo[0:rows_of(c), FIRST_SLOT[g] + n, :]),
                                       (gpt_hi[0:rows_of(c), c, :], gpt_lo[0:rows_of(c), c, :]))
                                      for n, c in enumerate(GROUP_CHUNKS[g])])
                        if g % 2:
                            mm.then_inc(g_o, 1)
                if duo(m, 0):
                    turn_probs(2 * d, 0, duo(m, -1))
                if duo(m, 2):
                    pe.wait_ge(g_xn, d + 3)
                    if duo(m, 0):
                        pe.wait_ge(g_shifted, 6 * d + 5)
                    for side in range(2):
                        for ct in range(CT):
                            mm = pe.transpose(banks[:, side, ct * P:(ct + 1) * P], xn[:, side, ct * P:(ct + 1) * P], ident[:, :])
                        mm.then_inc(g_xt_raw, 1)
                if duo(m, -1):
                    pe.wait_ge(g_ot_lo, 2 * d)
                    for side in range(2):
                        own = slice(side * P, (side + 1) * P)
                        product(pe, banks[:, 6 + side, :], [((ot_hi[:, ct, own], ot_lo[:, ct, own]), (go_hi[:, ct, :], go_lo[:, ct, :]))
                                                            for ct in range(CT)]).then_inc(g_out, 1)

            sweep(pe, -2, DUOS, DUO_LOOP, step)

        def of_round(w, rnd):
            return w[bass.ds(rnd, 1)].rearrange("r (t p) n -> p (r t) n", p=P)

        def dense_project_act(act, rnd):
            parts = [of_round(w, rnd)[:, :, q * C:(q + 1) * C] for w in (d_wk, d_wv) for q in range(2)]
            parts += [of_round(d_wq_t, rnd), of_round(d_wo, rnd)]
            act.dma_start(wst[0][:, :, :], parts[0]).then_inc(w_in[0], 16)
            act.dma_start(wst[1][:, :, :], parts[1]).then_inc(w_in[1], 16)
            for dst, src in ((tok_sb, token_c), (idx_i, d_idx[bass.ds(rnd, 1)].rearrange("r p n -> p (r n)")),
                             (m_sb[:, 0, :], mask_a), (m_sb[:, 1, :], mask_b),
                             (bo_sb, d_bo[bass.ds(rnd, 1)].rearrange("r p n -> p (r n)"))):
                act.dma_start(dst[:, :], src).then_inc(aux_in, 16)
            for n in range(4):
                for t in range(4 * n, 4 * n + 4):
                    act.wait_ge(proj_done, 16 * rnd + t + 1)
                    act.activation((k_t if t < PAIRS else v_t)[:, t % PAIRS, :], banks[:, t % 8, 0:BATCH * TOK],
                                   ACT.Copy).then_inc(proj_read, 1)
                act.dma_start(wst[n % 2][:, :, :], parts[n + 2]).then_inc(w_in[n % 2], 16)

        def dense_tiles_act(act, g0):
            def xt_part(i, u):
                act.wait_ge(d_xt_raw, g0 + i + 1)
                if there(i, -2):
                    act.wait_ge(d_scores, 3 * (g0 + i) - 3)
                act.activation(xt_hi[:, u % 2, :, :].rearrange("p t n -> p (t n)"), banks[:, 6, :],
                               ACT.Copy).then_inc(d_xt_hi, 1)

            def step(i, u):
                g = g0 + i
                if there(i, -2):
                    if there(i, -3):
                        act.wait_ge(d_out, g - 2)
                    for k, (c0, ncs) in enumerate(T_BANKS):
                        act.wait_ge(d_pt_raw, 3 * g - 5 + k)
                        copy_probs(act, k, 3 + k, pt_hi[:, :, :]).then_inc(d_pt_hi, 1)
                if isinstance(i, int) and i == 0:
                    xt_part(0, 0)
                if there(i, 1, 1):
                    xt_part(i + 1, u + 1)
                if there(i, 0):
                    act.wait_ge(d_shifted, g + 1)
                    act.activation(probs[:, u % 2, :], probs[:, u % 2, :], ACT.Exp, scale=DENSE_SCALE).then_inc(d_exp, 1)

            sweep(act, 0, TILES + 1, TILE_LOOP, step)

        def copy_probs(act, k, bank, dst):
            c0, ncs = T_BANKS[k]
            full = ncs if rows_of(c0 + ncs - 1) == P else ncs - 1
            ins = act.activation(dst[:, c0:c0 + full, :], banks[:, bank, 0:full * P].rearrange("p (c n) -> p c n", n=P), ACT.Copy)
            if full < ncs:
                c, r = c0 + full, rows_of(c0 + full)
                ins = act.activation(dst[0:r, c, :], banks[0:r, bank, full * P:ncs * P], ACT.Copy)
            return ins

        def rest_of_probs(dve, k, bank, hi, lo):
            c0, ncs = T_BANKS[k]
            full = ncs if rows_of(c0 + ncs - 1) == P else ncs - 1
            at = slice(c0, c0 + full)
            ins = dve.tensor_tensor(lo[:, at, :], banks[:, bank, 0:full * P].rearrange("p (c n) -> p c n", n=P),
                                    hi[:, at, :].bitcast(F32), ALU.subtract)
            if full < ncs:
                c, r = c0 + full, rows_of(c0 + full)
                ins = dve.tensor_tensor(lo[0:r, c, :], banks[0:r, bank, full * P:ncs * P],
                                        hi[0:r, c, :].bitcast(F32), ALU.subtract)
            return ins

        def group_tables_act(act, rnd):
            act.dma_start(wst[0][:, 0:2, :].rearrange("p a n -> p (a n)").rearrange("p (t n) -> p t n", t=XT),
                          of_round(g_wk, rnd)).then_inc(gw_in, 16)
            act.dma_start(wst[0][:, 2:4, :].rearrange("p a n -> p (a n)").rearrange("p (t n) -> p t n", t=XT),
                          of_round(g_wv, rnd)).then_inc(gw_in, 16)
            act.dma_start(wst[0][:, 4:8, :], of_round(g_wq, rnd)).then_inc(gw_in, 16)
            act.dma_start(wst[1][:, 0:4, :], of_round(g_wo, rnd)).then_inc(gw_in, 16)
            act.dma_start(norm_sb[:, :], g_norm[bass.ds(rnd, 1)].rearrange("r p n -> p (r n)")).then_inc(gw_in, 16)
            act.dma_start(select[:, :], select_c).then_inc(gw_in, 16)
            act.dma_start(spread[:, :], spread_c).then_inc(gw_in, 16)
            act.wait_ge(gw_in, 112 * rnd + 112)
            act.activation(go_hi[:, :, :], wst[1][:, 0:4, :], ACT.Copy).then_inc(g_hi, 1)
            for g in range(KV_HEADS):
                act.wait_ge(g_raw, 5 * rnd + g + 1)
                act.activation(gk_hi[:, g, :, :], gk_raw[:, :, :], ACT.Copy).then_inc(g_hi, 1)
            act.wait_ge(g_raw, 5 * rnd + 5)
            act.activation(gq_hi[:, :, :], gq_raw[:, :, :], ACT.Copy).then_inc(g_hi, 1)

        def duo_columns(ap, side):
            return ap[:, :, side * P:(side + 1) * P]

        def group_tiles_act(act, d0, stage):
            def probs_part(t, side):
                for k in range(len(T_BANKS)):
                    act.wait_ge(g_pt_raw, 3 * t + k + 1)
                    copy_probs(act, k, 3 + k, duo_columns(gpt_hi[:, :, :], side)).then_inc(g_pt_hi, 1)

            def exp(t, side):
                act.wait_ge(g_shifted, 3 * t + 3)
                act.activation(g_pr[:, side, :], g_pr[:, side, :], ACT.Exp, scale=GROUP_SCALE).then_inc(g_exp, 1)

            def step(m, u):
                d = d0 + m
                if duo(m, -1):
                    probs_part(2 * d - 1, 1)
                if duo(m, 0):
                    exp(2 * d, 0)
                if duo(m, 1):
                    for half_of in range(2):
                        act.wait_ge(g_q, 2 * d + 3 + half_of)
                        act.activation(qt_hi[:, (u + 1) % 2, 2 * half_of:2 * half_of + 2, :],
                                       banks[:, 6 + half_of, :].rearrange("p (g n) -> p g n", g=2), ACT.Copy).then_inc(g_qt_hi, 1)
                for half_of in range(2):
                    if duo(m, -1):
                        act.wait_ge(g_o, 2 * d - 1 + half_of)
                        act.activation(ot_hi[:, 2 * half_of:2 * half_of + 2, :],
                                       banks[:, 6 + half_of, :].rearrange("p (g n) -> p g n", g=2), ACT.Copy).then_inc(g_ot_hi, 1)
                    if half_of == 0 and duo(m, 0):
                        exp(2 * d + 1, 1)
                if duo(m, 0):
                    probs_part(2 * d, 0)
                if isinstance(m, int) and m <= 0:
                    for i in range(2 * m + 6, 2 * m + 8 if m < 0 else TILES):
                        act.wait_ge(x_in[i], 16 * stage + 16)
                if duo(m, 3):
                    if duo(m, 2):
                        act.wait_ge(g_rms, d + 3)
                    act.sem_inc(passed, 1)
                    for side in range(2):
                        act.activation(squares[:, side, :], slot(2 * m + 6 + side), ACT.Square,
                                       accum_out=ssq[:, side:side + 1]).then_inc(g_sq, 1)
                if duo(m, 2):
                    for side in range(2):
                        act.wait_ge(g_xt_raw, 2 * d + 5 + side)
                        act.activation(duo_columns(gxt_hi[:, :, :], side), banks[:, side, :].rearrange("p (t n) -> p t n", t=CT),
                                       ACT.Copy).then_inc(g_xt_hi, 1)
                if duo(m, 3):
                    act.wait_ge(g_rms, d + 4)
                    act.sem_inc(passed, 1)
                    for side in range(2):
                        ins = act.activation(xn[:, side, :], slot(2 * m + 6 + side), ACT.Copy, scale=rms[:, side:side + 1])
                    ins.then_inc(g_xn, 1)

            sweep(act, -3, DUOS, DUO_LOOP, step)

        BIAS_LINKS = 20

        def bias_dve(dve, rnd):
            links = 0

            def linked(ins):
                nonlocal links
                links += 1
                ins.then_inc(bias_link, 1)
                dve.wait_ge(bias_link, BIAS_LINKS * rnd + links)

            dve.wait_ge(aux_in, 80 * rnd + 80)
            linked(dve.tensor_copy(idx_f[:, 0:4], idx_i[:, :]))
            linked(dve.tensor_scalar(idx_f[:, 4:8], idx_f[:, 0:4], float(TOK), None, ALU.add))
            for n in range(8):
                linked(dve.tensor_scalar(hot[:, n, :], tok_sb[:, :], idx_f[:, n:n + 1], None, ALU.is_equal))
            for n, m in ((0, 1), (0, 4), (0, 5), (2, 3), (2, 6), (2, 7)):
                linked(dve.tensor_tensor(hot[:, n, :], hot[:, n, :], hot[:, m, :], ALU.max))
            linked(dve.tensor_tensor(hot[:, 0, :], hot[:, 0, :], hot[:, 2, :], ALU.is_gt))
            linked(dve.tensor_scalar(m_sb[:, :, :], m_sb[:, :, :], -1.0, 1.0, ALU.mult, ALU.add))

            def outer(dst, s, n):
                mask = m_sb[:, s, :].unsqueeze(2).broadcast_to([P, TILES, TOK])
                token = hot[:, n, :].unsqueeze(1).broadcast_to([P, TILES, TOK])
                return dve.tensor_tensor(dst[:, :, :], mask, token, ALU.mult)

            outer(bias8, 0, 0)
            linked(outer(bias_b, 1, 2))
            linked(dve.tensor_tensor(bias8[:, :, :], bias8[:, :, :], bias_b[:, :, :], ALU.add))
            assert links == BIAS_LINKS
            dve.tensor_scalar(bias8[:, :, :], bias8[:, :, :], -SUPPRESS / DENSE_SCALE, None, ALU.mult)

        def dense_tables_dve(dve, rnd, b):
            mask = half[:, :].unsqueeze(2).broadcast_to([P, 2, TOK])
            own = bass.ds(b * TOK, TOK)
            dve.tensor_tensor(k_bd[:, :, :].rearrange("p q (h k) -> p q h k", k=TOK),
                              k_t[:, :, own].unsqueeze(2).broadcast_to([P, PAIRS, 2, TOK]),
                              half[:, :].unsqueeze(1).unsqueeze(3).broadcast_to([P, PAIRS, 2, TOK]),
                              ALU.mult).then_inc(bd_ready, 1)
            dve.wait_ge(zero_done, rnd * BATCH + b + 1)
            for p in range(PAIRS):
                at = 2 * TOK * p - window_start(p)
                dve.tensor_tensor(v_bd[:, p, at:at + 2 * TOK].rearrange("p (h k) -> p h k", k=TOK),
                                  v_t[:, p, own].unsqueeze(1).broadcast_to([P, 2, TOK]), mask, ALU.mult).then_inc(bd_ready, 1)
            base = (rnd * BATCH + b) * GROUPS
            for n in range(CT * len(S_BANKS)):
                ct, (h0, nh) = n // len(S_BANKS), S_BANKS[n % len(S_BANKS)]
                cols = slice(h0 * TOK, (h0 + nh) * TOK)
                dve.wait_ge(tab_hi, base + n + 1)
                dve.tensor_tensor(kt_lo[:, ct, cols], banks[:, n % 8, 0:nh * TOK], kt_hi[:, ct, cols].bitcast(F32),
                                  ALU.subtract).then_inc(tab_lo, 1)
            for c in range(CHUNKS):
                n, r = CT * len(S_BANKS) + c, rows_of(c)
                dve.wait_ge(tab_hi, base + n + 1)
                dve.tensor_tensor(vt_lo[0:r, c, :], banks[0:r, n % 8, :], vt_hi[0:r, c, :].bitcast(F32),
                                  ALU.subtract).then_inc(tab_lo, 1)

        def slot(i):
            return x_ring[:, i, :] if isinstance(i, int) else x_ring[:, bass.ds(i, 1), :].rearrange("p a n -> p (a n)")

        def heads3(ap, nh):
            return ap.rearrange("p (h k) -> p h k", h=nh)

        def dense_tiles_dve(dve, g0, a0):
            def xt_rest(i, u):
                dve.wait_ge(d_xt_hi, g0 + i + 1)
                dve.tensor_tensor(xt_lo[:, u % 2, :, :].rearrange("p t n -> p (t n)"), banks[:, 6, :],
                                  xt_hi[:, u % 2, :, :].rearrange("p t n -> p (t n)").bitcast(F32), ALU.subtract).then_inc(d_xt_lo, 1)

            def step(i, u):
                g = g0 + i
                pr = probs[:, u % 2, :]
                if there(i, -3):
                    dve.wait_ge(d_out, g - 2)
                    dve.wait_ge(d_bo_added, g - 2)
                    dve.tensor_tensor(slot(i - 3), banks[:, 7, :], slot(i - 3), ALU.add).then_inc(x_updated, 1)
                if there(i, -2):
                    for k in range(3):
                        dve.wait_ge(d_pt_hi, 3 * g - 5 + k)
                        rest_of_probs(dve, k, 3 + k, pt_hi[:, :, :], pt_lo[:, :, :]).then_inc(d_pt_lo, 1)
                if isinstance(i, int) and i == 0:
                    xt_rest(0, 0)
                if there(i, 0):
                    bias = bias8[:, i, :] if isinstance(i, int) else bias8[:, bass.ds(i, 1), :].rearrange("p a n -> p (a n)")
                    for k, (h0, nh) in enumerate(S_BANKS):
                        dve.wait_ge(d_scores, 3 * g + k + 1)
                        dve.tensor_tensor(heads3(pr[:, h0 * TOK:(h0 + nh) * TOK], nh), heads3(banks[:, k, 0:nh * TOK], nh),
                                          bias.unsqueeze(1).broadcast_to([P, nh, TOK]), ALU.add).then_inc(d_biased, 1)
                if there(i, 1, 1):
                    xt_rest(i + 1, u + 1)
                if there(i, 0):
                    wide = heads3(pr, HEADS)
                    dve.wait_ge(d_biased, 3 * g + 3)
                    dve.tensor_reduce(row_max, wide, X, ALU.max).then_inc(d_max, 1)
                    dve.wait_ge(d_max, g + 1)
                    dve.tensor_tensor(wide, wide, row_max.unsqueeze(2).broadcast_to([P, HEADS, TOK]),
                                      ALU.subtract).then_inc(d_shifted, 1)
                    dve.wait_ge(d_exp, g + 1)
                    dve.tensor_reduce(row_sum, wide, X, ALU.add).then_inc(d_sum, 1)
                    dve.wait_ge(d_sum, g + 1)
                    dve.reciprocal(row_rcp, row_sum).then_inc(d_rcp, 1)
                    dve.wait_ge(d_rcp, g + 1)
                    dve.tensor_tensor(wide, wide, row_rcp.unsqueeze(2).broadcast_to([P, HEADS, TOK]),
                                      ALU.mult).then_inc(d_probs, 1)

            sweep(dve, 0, TILES + 2, TILE_LOOP, step)

        def group_tables_dve(dve, rnd):
            dve.wait_ge(g_proj, 3 * rnd + 1)
            dve.tensor_copy(k1[:, :], banks[:, 0, 0:BATCH * TOK]).then_inc(g_built, 1)
            for b in range(BATCH):
                dve.wait_ge(g_proj, 3 * rnd + b + 2)
                dve.tensor_copy(v1[0:TOK, b, :], banks[0:TOK, 4 + b, 0:P]).then_inc(g_built, 1)
            for g in range(KV_HEADS):
                dve.wait_ge(g_spread, KV_HEADS * rnd + g + 1)
                if g >= 1:
                    dve.wait_ge(g_lo, KV_HEADS * rnd + g)
                dve.tensor_tensor(gk_raw[:, :, :].rearrange("p b (r k) -> p b r k", k=TOK),
                                  banks[:, g, 0:BATCH * TOK].rearrange("p (b k) -> p b k", k=TOK).unsqueeze(2)
                                  .broadcast_to([P, BATCH, 4, TOK]),
                                  quarter[:, :].unsqueeze(1).unsqueeze(3).broadcast_to([P, BATCH, 4, TOK]),
                                  ALU.mult).then_inc(g_raw, 1)
                dve.wait_ge(g_hi, 6 * rnd + g + 2)
                dve.tensor_tensor(gk_lo[:, g, :, :], gk_raw[:, :, :], gk_hi[:, g, :, :].bitcast(F32), ALU.subtract).then_inc(g_lo, 1)
            dve.wait_ge(gw_in, 112 * rnd + 112)
            for ct in range(CT):
                ins = dve.tensor_scalar(gq_raw[:, ct, :], wst[0][:, 4 + ct, :], norm_sb[:, ct:ct + 1], None, ALU.mult)
            ins.then_inc(g_raw, 1)
            dve.tensor_tensor(go_lo[:, :, :], wst[1][:, 0:4, :], go_hi[:, :, :].bitcast(F32), ALU.subtract)
            dve.wait_ge(g_hi, 6 * rnd + 6)
            dve.tensor_tensor(gq_lo[:, :, :], gq_raw[:, :, :], gq_hi[:, :, :].bitcast(F32), ALU.subtract)
            dve.wait_ge(g_zero, rnd + 1)
            for b in range(BATCH):
                for c in range(CHUNKS):
                    r = rows_of(c)
                    n = b * CHUNKS + c
                    dve.wait_ge(g_rep, BATCH * CHUNKS * rnd + n + 1)
                    for g in range(KV_HEADS):
                        if c not in GROUP_CHUNKS[g]:
                            continue
                        s0 = FIRST_SLOT[g] + c - GROUP_CHUNKS[g][0]
                        ins = dve.tensor_tensor(gv_raw[0:r, b, s0, :].rearrange("p (r n) -> p r n", r=4),
                                                banks[0:r, 6 + n % 2, g * GROUP_D:(g + 1) * GROUP_D].unsqueeze(1).broadcast_to([r, 4, GROUP_D]),
                                                member[0:r, s0, :].unsqueeze(2).broadcast_to([r, 4, GROUP_D]), ALU.mult)
                    ins.then_inc(g_rep_read, 1)

        def group_tiles_dve(dve, b, visit, a0):
            d0 = visit * DUOS

            def shift(t, side):
                for k, (h0, nh) in enumerate(S_BANKS):
                    scores = heads3(banks[:, k, 0:nh * TOK], nh)
                    top = g_row_max[:, h0:h0 + nh]
                    dve.wait_ge(g_scores, 3 * t + k + 1)
                    dve.tensor_reduce(top, scores, X, ALU.max).then_inc(g_max, 1)
                    dve.wait_ge(g_max, 3 * t + k + 1)
                    dve.tensor_tensor(heads3(g_pr[:, side, h0 * TOK:(h0 + nh) * TOK], nh), scores,
                                      top.unsqueeze(2).broadcast_to([P, nh, TOK]), ALU.subtract).then_inc(g_shifted, 1)

            def denominators(t, side):
                dve.wait_ge(g_exp, t + 1)
                dve.tensor_reduce(g_sum[side], heads3(g_pr[:, side, :], HEADS), X, ALU.add).then_inc(g_sum_done, 1)
                dve.wait_ge(g_sum_done, t + 1)
                dve.reciprocal(g_rcp_of[side], g_sum[side]).then_inc(g_rcp, 1)

            def probs_rest(t, side):
                for k in range(len(T_BANKS)):
                    dve.wait_ge(g_pt_hi, 3 * t + k + 1)
                    rest_of_probs(dve, k, 3 + k, duo_columns(gpt_hi[:, :, :], side), duo_columns(gpt_lo[:, :, :], side)).then_inc(g_pt_lo, 1)

            def two_groups(ap, n):
                return ap.rearrange("p (g n) -> p g n", g=n)

            def q_rest(d, u, half_of):
                dve.wait_ge(g_qt_hi, 2 * d + 3 + half_of)
                own = slice(2 * half_of, 2 * half_of + 2)
                dve.tensor_tensor(qt_lo[:, (u + 1) % 2, own, :], two_groups(banks[:, 6 + half_of, :], 2),
                                  qt_hi[:, (u + 1) % 2, own, :].bitcast(F32), ALU.subtract).then_inc(g_qt_lo, 1)

            def step(m, u):
                d = d0 + m
                if duo(m, 0):
                    shift(2 * d, 0)
                if duo(m, -1):
                    probs_rest(2 * d - 1, 1)
                if duo(m, 1):
                    q_rest(d, u, 0)
                if duo(m, 0):
                    denominators(2 * d, 0)
                if duo(m, 1):
                    q_rest(d, u, 1)
                if duo(m, 0):
                    shift(2 * d + 1, 1)
                if duo(m, -1):
                    for half_of in range(2):
                        own = slice(2 * half_of, 2 * half_of + 2)
                        dve.wait_ge(g_ot_hi, 2 * d - 1 + half_of)
                        dve.tensor_tensor(ot_lo[:, own, :], two_groups(banks[:, 6 + half_of, :], 2),
                                          ot_hi[:, own, :].bitcast(F32), ALU.subtract).then_inc(g_ot_lo, 1)
                if duo(m, 0):
                    denominators(2 * d + 1, 1)
                    probs_rest(2 * d, 0)
                if duo(m, 2):
                    for side in range(2):
                        dve.wait_ge(g_xt_hi, 2 * d + 5 + side)
                        dve.tensor_tensor(duo_columns(gxt_lo[:, :, :], side), two_groups(banks[:, side, :], CT),
                                          duo_columns(gxt_hi[:, :, :], side).bitcast(F32), ALU.subtract).then_inc(g_xt_lo, 1)
                if duo(m, -1):
                    for side in range(2):
                        dve.wait_ge(g_out, 2 * d - 1 + side)
                        own = slot(2 * m - 2 + side)
                        dve.tensor_tensor(own, banks[:, 6 + side, :], own, ALU.add).then_inc(x_updated, 1)

            dve.wait_ge(g_v_hi, visit + 1)
            own = gv_raw[:, bass.ds(b, 1), :, :].rearrange("p a s n -> p (a s) n")
            dve.tensor_tensor(gv_lo[:, :, :], own, gv_hi[:, :, :].bitcast(F32), ALU.subtract).then_inc(g_v_lo, 1)
            sweep(dve, -2, DUOS, DUO_LOOP, step)


        def group_tiles_pool(pool, d0):
            def normalise(t, side):
                pool.wait_ge(g_rcp, t + 1)
                wide = heads3(g_pr[:, side, :], HEADS)
                pool.tensor_tensor(wide, wide, g_rcp_of[side].unsqueeze(2).broadcast_to([P, HEADS, TOK]),
                                   ALU.mult).then_inc(g_probs, 1)

            def step(m, u):
                d = d0 + m
                if duo(m, 0):
                    normalise(2 * d, 0)
                    normalise(2 * d + 1, 1)
                if duo(m, 3):
                    pool.wait_ge(g_sq, 2 * d + 8)
                    if duo(m, 2):
                        pool.wait_ge(g_xn, d + 3)
                    pool.sem_inc(passed, 1)
                    pool.tensor_scalar(mean_sq, ssq, 1.0 / C, EPS, ALU.mult, ALU.add).then_inc(g_var, 1)
                    pool.wait_ge(g_var, d + 4)
                    pool.tensor_tensor(rms, mean_sq, exponent, ALU.pow).then_inc(g_rms, 1)

            sweep(pool, -3, DUOS - 1, DUO_LOOP, step)

        block = ctx.enter_context(nc.Block())

        @block.tensor
        def _(pe):
            pe.wait_ge(const_in, 16 * 5)
            with pe.Fori(0, ROUNDS) as rnd:
                for n in range(4):
                    pe.wait_ge(w_in[n % 2], 48 * rnd + 16 * (n // 2 + 1))
                    for m in range(4):
                        t = 4 * n + m
                        if t >= 8:
                            pe.wait_ge(proj_read, 16 * rnd + t - 7)
                        for kt in range(XT):
                            mm = pe.matmul(banks[:, t % 8, 0:BATCH * TOK], wst[n % 2][:, kt, m * P:(m + 1) * P],
                                           ctx_sb[:, kt, :], start=kt == 0, stop=kt == XT - 1)
                        mm.then_inc(proj_done, 1)
                stage_end(pe, rnd, 0)
                with pe.Fori(0, BATCH) as b:
                    dense_tables_pe(pe, rnd, b)
                    stage_end(pe, rnd, 2 * b + 1)
                    dense_tiles_pe(pe, (rnd * BATCH + b) * TILES, (rnd * 2 * BATCH + b) * TILES)
                    stage_end(pe, rnd, 2 * b + 2)
                group_tables_pe(pe, rnd)
                stage_end(pe, rnd, 5)
                with pe.Fori(0, BATCH) as b:
                    group_tiles_pe(pe, b, rnd * BATCH + b, (rnd * 2 * BATCH + b + BATCH) * TILES)
                    stage_end(pe, rnd, b + 6)

        @block.scalar
        def _(act):
            with act.Fori(0, ROUNDS) as rnd:
                dense_project_act(act, rnd)
                stage_end(act, rnd, 0)
                with act.Fori(0, BATCH) as b:
                    base = (rnd * BATCH + b) * GROUPS
                    for n in range(CT * len(S_BANKS)):
                        ct, (h0, nh) = n // len(S_BANKS), S_BANKS[n % len(S_BANKS)]
                        act.wait_ge(tab_done, base + n + 1)
                        act.activation(kt_hi[:, ct, h0 * TOK:(h0 + nh) * TOK], banks[:, n % 8, 0:nh * TOK],
                                       ACT.Copy).then_inc(tab_hi, 1)
                    for c in range(CHUNKS):
                        n, r = CT * len(S_BANKS) + c, rows_of(c)
                        act.wait_ge(tab_done, base + n + 1)
                        act.activation(vt_hi[0:r, c, :], banks[0:r, n % 8, :], ACT.Copy).then_inc(tab_hi, 1)
                    stage_end(act, rnd, 2 * b + 1)
                    dense_tiles_act(act, (rnd * BATCH + b) * TILES)
                    stage_end(act, rnd, 2 * b + 2)
                group_tables_act(act, rnd)
                stage_end(act, rnd, 5)
                with act.Fori(0, BATCH) as b:
                    act.activation(gv_hi[:, :, :], gv_raw[:, bass.ds(b, 1), :, :].rearrange("p a s n -> p (a s) n"),
                                   ACT.Copy).then_inc(g_v_hi, 1)
                    group_tiles_act(act, (rnd * BATCH + b) * DUOS, rnd * 2 * BATCH + b + BATCH)
                    stage_end(act, rnd, b + 6)

        @block.vector
        def _(dve):
            dve.wait_ge(const_in, 16 * 5)
            with dve.Fori(0, ROUNDS) as rnd:
                bias_dve(dve, rnd)
                stage_end(dve, rnd, 0)
                with dve.Fori(0, BATCH) as b:
                    dense_tables_dve(dve, rnd, b)
                    stage_end(dve, rnd, 2 * b + 1)
                    dense_tiles_dve(dve, (rnd * BATCH + b) * TILES, (rnd * 2 * BATCH + b) * TILES)
                    stage_end(dve, rnd, 2 * b + 2)
                group_tables_dve(dve, rnd)
                stage_end(dve, rnd, 5)
                with dve.Fori(0, BATCH) as b:
                    group_tiles_dve(dve, b, rnd * BATCH + b, (rnd * 2 * BATCH + b + BATCH) * TILES)
                    stage_end(dve, rnd, b + 6)

        @block.gpsimd
        def _(pool):
            pool.memset(exponent, -0.5).then_inc(exponent_set, 1)
            pool.wait_ge(exponent_set, 1)
            with pool.Fori(0, ROUNDS) as rnd:
                stage_end(pool, rnd, 0)
                with pool.Fori(0, BATCH) as b:
                    pool.memset(v_bd[:, :, :], 0.0).then_inc(zero_done, 1)
                    stage_end(pool, rnd, 2 * b + 1)
                    stage, g = rnd * 2 * BATCH + b, (rnd * BATCH + b) * TILES
                    for i in range(TILES):
                        pool.wait_ge(x_in[i], 16 * stage + 16)
                        if i >= 2:
                            pool.wait_ge(d_xt_raw, g + i - 1)
                        pool.sem_inc(passed, 1)
                        pool.tensor_copy(xs[:, i % 2, :], x_ring[:, i, :]).then_inc(xs_ready, 1)
                        pool.tensor_tensor(x_ring[:, i, :], x_ring[:, i, :], bo_sb[:, :], ALU.add).then_inc(d_bo_added, 1)
                    stage_end(pool, rnd, 2 * b + 2)
                pool.memset(gv_raw[:, :, SLOTS - 1, :], 0.0).then_inc(g_zero, 1)
                stage_end(pool, rnd, 5)
                with pool.Fori(0, BATCH) as b:
                    group_tiles_pool(pool, (rnd * BATCH + b) * DUOS)
                    stage_end(pool, rnd, b + 6)

        @block.sync
        def _(sp):
            for dst, src in ((ident[:, :], ident_c), (half[:, :], half_c), (quarter[:, :], quarter_c), (member[:, :, :], member_c)):
                sp.dma_start(dst, src).then_inc(const_in, 16)
            sp.dma_start(ctx_sb[:, :, :], ctx_t.rearrange("(t p) n -> p t n", p=P)).then_inc(const_in, 16)
            x_t = x.rearrange("b (t p) n -> b t p n", p=P)
            out_t = out.rearrange("b (t p) n -> b t p n", p=P)
            for i in range(TILES):
                sp.dma_start(x_ring[:, i, :], x_t[0, i]).then_inc(x_in[i], 16)

            def stage(s, dst, src, src_ready=None):
                def load(i):
                    sp.wait_ge(x_out[i], 16 * s + 16)
                    sp.dma_start(x_ring[:, i, :], src[i]).then_inc(x_in[i], 16)

                for i in range(TILES):
                    sp.wait_ge(x_updated, TILES * s + i + 1)
                    sp.dma_start(dst[i], x_ring[:, i, :]).then_inc(x_out[i], 16)
                    if src is not None and i >= 1:
                        load(i - 1)
                if src is not None:
                    load(TILES - 1)

            stage(0, x_mid[0], x_t[1])
            stage(1, x_mid[1], x_mid[0])
            with sp.Fori(1, ROUNDS * 2 - 1) as t:
                stage(2 * t, x_mid[0], x_mid[1])
                stage(2 * t + 1, x_mid[1], x_mid[0])
            stage(ROUNDS * 4 - 2, out_t[0], x_mid[1])
            stage(ROUNDS * 4 - 1, out_t[1], None)
            for i in range(TILES):
                sp.wait_ge(x_out[i], 16 * ROUNDS * 4)


def constants():
    rows = np.arange(P)
    keys = np.arange(KEYS)
    member = np.zeros((P, SLOTS, 4), np.float32)
    for g, chunks in enumerate(GROUP_CHUNKS):
        for n, c in enumerate(chunks):
            member[:, FIRST_SLOT[g] + n] = (c * P + rows[:, None]) // TOK == 4 * g + np.arange(4)
    return {
        "ident_c": np.eye(P, dtype=np.float32),
        "half_c": (rows[:, None] // DENSE_D == np.arange(2)).astype(np.float32),
        "quarter_c": (rows[:, None] // GROUP_D == np.arange(4)).astype(np.float32),
        "member_c": member,
        "select_c": (keys[None, :] % TOK == np.arange(TOK)[:, None]).astype(np.float32),
        "spread_c": np.concatenate([(rows[:, None] == g * GROUP_D + rows[None, :] % GROUP_D).astype(np.float32)
                                    for g in range(KV_HEADS)], axis=1),
        "token_c": np.ascontiguousarray(np.broadcast_to(np.arange(TOK, dtype=np.float32), (P, TOK))),
    }


def kernel(**inputs):
    import concourse.bacc as bacc
    from concourse.bass_utils import run_bass_kernel_spmd as run

    a = {k: np.asarray(v) for k, v in inputs.items()}

    def both(name):
        return np.stack([a[f"L{n}_xattn_{name}"] for n in (0, 2)])

    def both_g(name):
        return np.stack([a[f"L{n}_xattn_{name}"] for n in (1, 3)])

    def on_rows(v):
        return np.broadcast_to(v[:, None, :], (v.shape[0], P, v.shape[1]))

    arrays = {
        "x": a["x"],
        "ctx_t": a["ctx_2048"].reshape(BATCH * TOK, CTX).T,
        "mask_a": a["mask_S_fk1"].reshape(TILES, P).T,
        "mask_b": a["mask_S_fk0"].reshape(TILES, P).T,
        "d_wq_t": both("Wq").transpose(0, 2, 1),
        "d_wk": both("Wk"),
        "d_wv": both("Wv"),
        "d_wo": both("Wo"),
        "d_bo": on_rows(both("bo")),
        "d_idx": on_rows(np.concatenate([both("token_indices_A"), both("token_indices_B")], axis=1)),
        "g_wq": both_g("wq"),
        "g_wk": both_g("wk"),
        "g_wv": both_g("wv"),
        "g_wo": both_g("wo"),
        "g_norm": both_g("norm_w").reshape(ROUNDS, CT, P).transpose(0, 2, 1),
        **constants(),
    }
    arrays = {k: np.ascontiguousarray(v) for k, v in arrays.items()}
    nc = bacc.Bacc("TRN2", target_bir_lowering=False, num_devices=1)
    args = [nc.dram_tensor(k, v.shape, mybir.dt.from_np(v.dtype), kind="ExternalInput").ap() for k, v in arrays.items()]
    out = nc.dram_tensor("out", (BATCH, ROWS, C), F32, kind="ExternalOutput").ap()
    build(nc, *args, out)
    r = run(nc, [arrays], core_ids=[0])
    return r.results[0]["out"]
```

```python
from contextlib import ExitStack

import numpy as np
import concourse.bass as bass
from concourse import mybir

ALU = mybir.AluOpType
ACT = mybir.ActivationFunctionType
X = mybir.AxisListType.X
F32 = mybir.dt.float32
F32R = mybir.dt.float32r
I32 = mybir.dt.int32

P = 128
ROUNDS = 2
BATCH, ROWS, C = 2, 2048, 512
TOK, CTX = 77, 1024
HEADS = 16
DENSE_D, GROUP_D, KV_HEADS = 64, 32, 4
INNER = HEADS * DENSE_D
KEYS = HEADS * TOK
TILES = ROWS // P
CT, XT = C // P, CTX // P
PAIRS = INNER // P
CHUNKS = -(-KEYS // P)
BANK = 512
DUOS = TILES // 2
UNROLL = 2
TILE_LOOP = (3, TILES - 3)
ALL_DUOS = BATCH * DUOS
DUO_LOOPS = [(DUOS * b + 1, DUOS * b + DUOS - 3) for b in range(BATCH)]
AHEAD = 4
EPS = 1e-5
SUPPRESS = 20.0
DENSE_SCALE = DENSE_D ** -0.5
GROUP_SCALE = float(np.float32(1.0) / np.sqrt(GROUP_D).astype(np.float32))

S_BANKS = [(0, 6), (6, 6), (12, 4)]
T_BANKS = [(0, 4), (4, 4), (8, 2)]


def rows_of(c):
    return min(P, KEYS - c * P)


def pairs_of(c):
    return range(c * P // (2 * TOK), (c * P + rows_of(c) - 1) // (2 * TOK) + 1)


GROUP_CHUNKS = [range(g * 4 * TOK // P, ((g + 1) * 4 * TOK - 1) // P + 1) for g in range(KV_HEADS)]
FIRST_SLOT = [sum(len(x) for x in GROUP_CHUNKS[:g]) for g in range(KV_HEADS + 1)]
SLOTS = FIRST_SLOT[KV_HEADS]


def window_start(p):
    return p * 2 * TOK // P * P


WINDOWS = [-(-(p + 1) * 2 * TOK // P) * P - window_start(p) for p in range(PAIRS)]
WINDOW_AT = [sum(WINDOWS[:p]) for p in range(PAIRS + 1)]


def build(nc, x, ctx_t, mask_a, mask_b, d_wq_t, d_wk, d_wv, d_wo, d_bo, d_idx,
          g_wq, g_wk, g_wv, g_wo, g_norm, ident_c, half_c, quarter_c, member_c, select_c, spread_c, token_c, out):
    ctx = ExitStack()
    with ctx:
        def sem(name):
            return ctx.enter_context(nc.semaphore(name))

        def sb(name, shape, dt=F32, scope=ctx):
            return scope.enter_context(nc.sbuf_tensor(name, shape, dt))

        ident = sb("ident", [P, P])
        half = sb("half", [P, 2])
        quarter = sb("quarter", [P, 4])
        member = sb("member", [P, SLOTS, 4])
        select = sb("select", [TOK, TOK + P], F32R)
        spread = sb("spread", [P, KV_HEADS * P], F32R)
        norm_sb = sb("norm_sb", [P, CT])
        ctx_sb = sb("ctx_sb", [P, XT, BATCH * TOK])
        x_ring = sb("x_ring", [P, TILES, C])
        wst = [sb("wst0", [P, XT, C])]
        with ExitStack() as s:
            wst.append(sb("wst1", [P, XT, C], F32, s))
        with ExitStack() as s:
            qt_hi = sb("qt_hi", [P, 2, CT, 2 * P], F32R, s)
            qt_lo = sb("qt_lo", [P, 2, CT, 2 * P], F32R, s)
        sb("wst1_place", [P, XT, C])
        small = sb("small", [P, 88])
        banks = ctx.enter_context(nc.psum_tensor("banks", [P, 8, BANK], F32))

        with ExitStack() as s:
            kt_hi = sb("kt_hi", [P, CT, KEYS], F32R, s)
            kt_lo = sb("kt_lo", [P, CT, KEYS], F32R, s)
            vt_hi = sb("vt_hi", [P, CHUNKS, C], F32R, s)
            vt_lo = sb("vt_lo", [P, CHUNKS, C], F32R, s)
        with ExitStack() as s:
            gq_hi = sb("gq_hi", [P, CT, C], F32R, s)
            gq_lo = sb("gq_lo", [P, CT, C], F32R, s)
            go_hi = sb("go_hi", [P, CT, C], F32R, s)
            go_lo = sb("go_lo", [P, CT, C], F32R, s)
            gk = sb("gk", [P, KV_HEADS, 2, BATCH, 4 * TOK], F32R, s)
            gv = sb("gv", [P, BATCH, SLOTS, 2, P], F32R, s)
        with ExitStack() as s:
            select_raw = sb("select_raw", [TOK, TOK + P], F32, s)
            spread_raw = sb("spread_raw", [P, KV_HEADS * P], F32, s)
            tok_sb = sb("tok_sb", [P, TOK], F32, s)
            idx_i = sb("idx_i", [P, 4], I32, s)
            idx_f = sb("idx_f", [P, 8], F32, s)
            hot = sb("hot", [P, 8, TOK], F32, s)
            bias_b = sb("bias_b", [P, TILES, TOK], F32, s)
            m_sb = sb("m_sb", [P, 2, TILES], F32, s)
        sb("tables_place", [P, 2 * CT * KEYS + 2 * CHUNKS * C])

        with ExitStack() as s:
            bias8 = sb("bias8", [P, TILES, TOK], F32, s)
            bo_sb = sb("bo_sb", [P, C], F32, s)
            k_t = sb("k_t", [P, PAIRS, BATCH * TOK], F32, s)
            v_t = sb("v_t", [P, PAIRS, BATCH * TOK], F32, s)
            k_bd = sb("k_bd", [P, PAIRS, 2 * TOK], F32, s)
        with ExitStack() as s:
            ot_hi = sb("ot_hi", [P, CT, 2 * P], F32R, s)
            ot_lo = sb("ot_lo", [P, CT, 2 * P], F32R, s)
            g_pr = sb("g_pr", [P, 2, KEYS], F32, s)
            squares = sb("squares", [P, 2, C], mybir.dt.bfloat16, s)
        sb("layer_place", [P, TILES * TOK + C + 2 * PAIRS * BATCH * TOK + PAIRS * 2 * TOK])

        with ExitStack() as s:
            xt_hi = sb("xt_hi", [P, 2, CT, P], F32R, s)
            xt_lo = sb("xt_lo", [P, 2, CT, P], F32R, s)
            pt_hi = sb("pt_hi", [P, CHUNKS, P], F32R, s)
            pt_lo = sb("pt_lo", [P, CHUNKS, P], F32R, s)
            probs = sb("probs", [P, 2, KEYS], F32, s)
            xs = sb("xs", [P, 2, C], F32, s)
        with ExitStack() as s:
            sb("before_probs", [P, 2 * 2 * CT * P + 2 * CHUNKS * P], F32, s)
            v_bd = sb("v_bd", [P, WINDOW_AT[PAIRS]], F32, s)
        with ExitStack() as s:
            gxt_hi = sb("gxt_hi", [P, CT, 2 * P], F32R, s)
            gxt_lo = sb("gxt_lo", [P, CT, 2 * P], F32R, s)
            gpt_hi = sb("gpt_hi", [P, CHUNKS, 2 * P], F32R, s)
            gpt_lo = sb("gpt_lo", [P, CHUNKS, 2 * P], F32R, s)
            xn = sb("xn", [P, 2, C], F32, s)
        with ExitStack() as s:
            sb("before_kv", [P, 2 * 2 * CT * P + 2 * CHUNKS * P], F32, s)
            k1 = sb("k1", [P, 2, BATCH * TOK], F32R, s)
            v1 = sb("v1", [P, BATCH, 2, P], F32R, s)
        sb("work_place", [P, 2 * CT * 2 * P + 2 * CHUNKS * 2 * P + 2 * C])

        row_max = small[:, 0:16]
        row_sum = small[:, 16:32]
        row_rcp = small[:, 32:48]
        g_sum = [small[:, 16:32], small[:, 0:16]]
        g_rcp_of = [small[:, 32:48], small[:, 56:72]]
        g_row_max = small[:, 72:88]
        ssq = small[:, 48:50]
        rms = small[:, 50:52]
        mean_sq = small[:, 52:54]
        exponent = small[:, 54:56]

        x_mid = nc.dram_tensor("x_mid", [BATCH, TILES, P, C], F32, kind="Internal").ap()

        const_in = sem("const_in")
        passed = sem("passed")
        round_done = sem("round_done")
        x_there = sem("x_there")
        x_in = [sem(f"x_in{i}") for i in range(TILES)]
        x_out = [sem(f"x_out{i}") for i in range(TILES)]
        xs_ready = sem("xs_ready")
        x_updated = sem("x_updated")
        w_in = [sem("w_in0"), sem("w_in1")]
        w_first = sem("w_first")
        gw_in = sem("gw_in")
        aux_in = sem("aux_in")
        proj_done, proj_read = sem("proj_done"), sem("proj_read")
        kbd_ready, vbd_ready, zero_done = sem("kbd_ready"), sem("vbd_ready"), sem("zero_done")
        kt_raw, kt_hi_made, kt_lo_made = sem("kt_raw"), sem("kt_hi_made"), sem("kt_lo_made")
        vt_raw, vt_hi_made, vt_lo_made = sem("vt_raw"), sem("vt_hi_made"), sem("vt_lo_made")
        bias_link = sem("bias_link")
        d_xt_raw, d_xt_hi, d_xt_lo = sem("d_xt_raw"), sem("d_xt_hi"), sem("d_xt_lo")
        d_scores, d_biased, d_max = sem("d_scores"), sem("d_biased"), sem("d_max")
        d_shifted, d_exp, d_sum, d_rcp = sem("d_shifted"), sem("d_exp"), sem("d_sum"), sem("d_rcp")
        d_probs, d_bo_added = sem("d_probs"), sem("d_bo_added")
        d_pt_raw, d_pt_hi, d_pt_lo = sem("d_pt_raw"), sem("d_pt_hi"), sem("d_pt_lo")
        d_out = sem("d_out")
        consts_raw = sem("consts_raw")
        g_proj, kv_hi, kv_lo = sem("g_proj"), sem("kv_hi"), sem("kv_lo")
        k_spread, k_built_dve, k_built_act = sem("k_spread"), sem("k_built_dve"), sem("k_built_act")
        v_spread, v_built = sem("v_spread"), sem("v_built")
        wq_hi, wq_lo, wo_hi, wo_lo = sem("wq_hi"), sem("wq_lo"), sem("wo_hi"), sem("wo_lo")
        exponent_set = sem("exponent_set")
        g_sq, g_var, g_rms, g_xn = sem("g_sq"), sem("g_var"), sem("g_rms"), sem("g_xn")
        g_xt_raw, g_xt_hi, g_xt_lo = sem("g_xt_raw"), sem("g_xt_hi"), sem("g_xt_lo")
        g_q, g_qt_hi, g_qt_lo = sem("g_q"), sem("g_qt_hi"), sem("g_qt_lo")
        g_scores, g_max, g_shifted, g_exp = sem("g_scores"), sem("g_max"), sem("g_shifted"), sem("g_exp")
        g_sum_done, g_rcp, g_probs = sem("g_sum_done"), sem("g_rcp"), sem("g_probs")
        g_pt_raw, g_pt_hi, g_pt_lo = sem("g_pt_raw"), sem("g_pt_hi"), sem("g_pt_lo")
        g_o, g_ot_hi, g_ot_lo = sem("g_o"), sem("g_ot_hi"), sem("g_ot_lo")
        g_out = sem("g_out")

        def round_end(eng, rnd):
            eng.drain().then_inc(round_done, 1)
            eng.wait_ge(round_done, 4 * rnd + 4)
            eng.sem_inc(passed, 1)

        def sweep(eng, first, last, loops, step):
            i = first
            for lo, hi in loops:
                while i < lo:
                    step(i, i)
                    i += 1
                with eng.Fori(0, (hi - lo) // UNROLL) as j:
                    for u in range(UNROLL):
                        step(UNROLL * j + (lo + u), lo + u)
                i = hi
            while i <= last:
                step(i, i)
                i += 1

        def only(i, n):
            return isinstance(i, int) and i == n

        def there(i, d, lo=0, n=TILES):
            return not isinstance(i, int) or lo <= i + d < n

        def o_bank(m):
            return 6 if duo(m, 0) else 0

        def duo(m, d):
            return there(m, d, 0, ALL_DUOS)

        def product(pe, dst, pairs, first=True, last=True, check=True):
            n = 3 * len(pairs)
            at = 0
            for (a_hi, a_lo), (b_hi, b_lo) in pairs:
                for a, b in ((a_hi, b_hi), (a_hi, b_lo), (a_lo, b_hi)):
                    mm = pe.matmul(dst, a, b, start=first and at == 0, stop=last and at == n - 1,
                                   skip_group_check=not check)
                    at += 1
            return mm

        GROUPS = [(ct, h0, nh) for ct in range(CT) for h0, nh in S_BANKS]
        KT_BANKS = (0, 1, 2, 6)
        VT_BANKS = (3, 4, 5)
        HALF = len(GROUPS) // 2
        LATE = min(c for c in range(CHUNKS) if WINDOW_AT[pairs_of(c)[0]] >= KEYS)
        X_AFTER = (2, 5)

        def key_table_pe(pe, visit, numbers):
            for n in numbers:
                ct, h0, nh = GROUPS[n]
                if n >= len(KT_BANKS):
                    pe.wait_ge(kt_lo_made, visit * len(GROUPS) + n - len(KT_BANKS) + 1)
                for p in range(h0 // 2, (h0 + nh) // 2):
                    at = (p - h0 // 2) * 2 * TOK
                    mm = pe.matmul(banks[:, KT_BANKS[n % 4], at:at + 2 * TOK], wst[0][:, p, ct * P:(ct + 1) * P],
                                   k_bd[:, p, :], start=True, stop=True)
                mm.then_inc(kt_raw, 1)

        def value_table_pe(pe, visit, chunks):
            for c in chunks:
                if c >= len(VT_BANKS):
                    pe.wait_ge(vt_lo_made, visit * CHUNKS + c - len(VT_BANKS) + 1)
                for p in pairs_of(c):
                    at = WINDOW_AT[p] + c * P - window_start(p)
                    mm = pe.matmul(banks[0:rows_of(c), VT_BANKS[c % 3], :], v_bd[:, at:at + rows_of(c)], wst[1][:, p, :],
                                   start=p == pairs_of(c)[0], stop=p == pairs_of(c)[-1])
                mm.then_inc(vt_raw, 1)

        both_v = banks[0:TOK, 6, 0:BATCH * P].rearrange("p (b n) -> p b n", b=BATCH)

        def group_project_k(pe, rnd):
            pe.wait_ge(gw_in, 80 * rnd + 80)
            for kt in range(XT):
                mm = pe.matmul(banks[:, 2, 0:BATCH * TOK], kv_weights(0)[:, kt, :], ctx_sb[:, kt, :], start=kt == 0, stop=kt == XT - 1)
            mm.then_inc(g_proj, 1)

        def group_project_v(pe):
            for b in range(BATCH):
                for kt in range(XT):
                    mm = pe.matmul(banks[0:TOK, 6, b * P:(b + 1) * P], ctx_sb[:, kt, b * TOK:(b + 1) * TOK], kv_weights(1)[:, kt, :],
                                   start=kt == 0, stop=kt == XT - 1)
            mm.then_inc(g_proj, 1)

        def dense_pe(pe, rnd, b, start_group):
            visit = rnd * BATCH + b
            g0, a0 = visit * TILES, (rnd * 2 * BATCH + b) * TILES

            def turn_x(i, u):
                pe.wait_ge(xs_ready, g0 + i + 1)
                for ct in range(CT):
                    mm = pe.transpose(banks[:, 6, ct * P:(ct + 1) * P], xs[:, u % 2, ct * P:(ct + 1) * P], ident[:, :])
                mm.then_inc(d_xt_raw, 1)

            def step(i, u):
                g = g0 + i
                if there(i, -2):
                    if only(i, 2):
                        pe.wait_ge(vt_lo_made, CHUNKS * (visit + 1))
                    pe.wait_ge(d_probs, g - 1)
                    for k, (c0, ncs) in enumerate(T_BANKS):
                        if there(i, -3):
                            pe.wait_ge(d_pt_lo, 3 * g - 8 + k)
                        for c in range(c0, c0 + ncs):
                            mm = pe.transpose(banks[0:rows_of(c), 3 + k, (c - c0) * P:(c - c0 + 1) * P],
                                              probs[:, u % 2, c * P:c * P + rows_of(c)], ident[:, :])
                        mm.then_inc(d_pt_raw, 1)
                if only(i, TILES) and b < BATCH - 1:
                    pe.wait_ge(kbd_ready, visit + 2)
                    pe.wait_ge(d_biased, 3 * (g0 + TILES))
                    key_table_pe(pe, visit + 1, range(HALF))
                if only(i, TILES + 1) and b < BATCH - 1:
                    key_table_pe(pe, visit + 1, range(HALF, len(GROUPS)))
                if only(i, TILES) and b == BATCH - 1:
                    pe.wait_ge(d_biased, 3 * (g0 + TILES))
                    group_project_k(pe, rnd)
                if only(i, TILES + 1) and b == BATCH - 1:
                    group_project_v(pe)
                    start_group()
                if only(i, 1):
                    turn_x(2, 2)
                if there(i, 0):
                    pe.wait_ge(d_xt_lo, g + 1)
                    for k, (h0, nh) in enumerate(S_BANKS):
                        if there(i, -1):
                            pe.wait_ge(d_biased, 3 * g - 2 + k)
                        cols = slice(h0 * TOK, (h0 + nh) * TOK)
                        product(pe, banks[:, k, 0:nh * TOK],
                                [((xt_hi[:, u % 2, ct, :], xt_lo[:, u % 2, ct, :]), (kt_hi[:, ct, cols], kt_lo[:, ct, cols]))
                                 for ct in range(CT)]).then_inc(d_scores, 1)
                if only(i, 0):
                    value_table_pe(pe, visit, range(LATE, CHUNKS))
                if there(i, 1, 3):
                    turn_x(i + 1, u + 1)
                if there(i, -2):
                    if there(i, -3) or b:
                        pe.wait_ge(x_updated, a0 + i - 2)
                    for c in range(CHUNKS):
                        if c % 4 == 0:
                            pe.wait_ge(d_pt_lo, 3 * g - 5 + c // 4)
                        r = rows_of(c)
                        mm = product(pe, banks[:, 7, :], [((pt_hi[0:r, c, :], pt_lo[0:r, c, :]), (vt_hi[0:r, c, :], vt_lo[0:r, c, :]))],
                                     first=c == 0, last=c == CHUNKS - 1)
                    mm.then_inc(d_out, 1)

            if b == 0:
                pe.wait_ge(w_in[0], 48 * (rnd + 1))
                pe.wait_ge(kbd_ready, visit + 1)
                pe.wait_ge(proj_read, 16 * rnd + 16)
                key_table_pe(pe, visit, range(len(GROUPS)))
            if b == 0:
                pe.wait_ge(w_in[1], 48 * (rnd + 1))
            pe.wait_ge(vbd_ready, visit + 1)
            value_table_pe(pe, visit, range(0, X_AFTER[0]))
            pe.wait_ge(kt_lo_made, len(GROUPS) * (visit + 1))
            turn_x(0, 0)
            value_table_pe(pe, visit, range(X_AFTER[0], X_AFTER[1]))
            pe.wait_ge(d_xt_lo, g0 + 1)
            turn_x(1, 1)
            value_table_pe(pe, visit, range(X_AFTER[1], LATE))
            sweep(pe, 0, TILES + 1, [TILE_LOOP], step)

        K_BANKS = (5, 2, 3, 4)
        V_BANKS = 3
        V_LOADS = CHUNKS // 2

        def kv_weights(n):
            return wst[0][:, 2 * n:2 * n + 2, :].rearrange("p a n -> p (a n)").rearrange("p (t n) -> p t n", t=XT)

        def group_pe(pe, rnd, a0):
            d0 = rnd * ALL_DUOS

            def spread_k():
                pe.wait_ge(kv_lo, 2 * rnd + 2)
                for g in range(KV_HEADS):
                    pe.matmul(banks[:, K_BANKS[g], 0:2 * BATCH * TOK], spread[:, g * P:(g + 1) * P],
                              k1[:, :, :].rearrange("p a n -> p (a n)"), start=True, stop=True).then_inc(k_spread, 1)

            def spread_v(numbers):
                for at in numbers:
                    b, n = at // V_LOADS, at % V_LOADS
                    if at < V_BANKS:
                        if at < 2:
                            pe.wait_ge(k_built_act, 2 * rnd + at + 1)
                        else:
                            pe.wait_ge(k_built_dve, 2 * rnd + 1)
                    else:
                        pe.wait_ge(v_built, BATCH * V_LOADS * rnd + at - V_BANKS + 1)
                    for c in (2 * n, 2 * n + 1):
                        r = rows_of(c)
                        mm = pe.matmul(banks[0:r, 3 + at % V_BANKS, c % 2 * 2 * P:(c % 2 + 1) * 2 * P],
                                       select[:, c * P % TOK:c * P % TOK + r],
                                       v1[0:TOK, b, :, :].rearrange("p a n -> p (a n)"), start=True, stop=True)
                    mm.then_inc(v_spread, 1)

            def scores(m, u, side):
                d = d0 + m
                for k, (h0, nh) in enumerate(S_BANKS):
                    if side == 0 and duo(m, -1):
                        pe.wait_ge(g_shifted, 6 * d - 2 + k)
                    if side == 1:
                        pe.wait_ge(g_shifted, 6 * d + 1 + k)
                    for grp in range(h0 // 4, -(-(h0 + nh) // 4)):
                        lo, hi = max(h0, 4 * grp), min(h0 + nh, 4 * grp + 4)
                        cols = slice((lo - 4 * grp) * TOK, (hi - 4 * grp) * TOK)
                        own = slice(side * P, (side + 1) * P)
                        mm = product(pe, banks[:, k, (lo - h0) * TOK:(hi - h0) * TOK],
                                     [((qt_hi[:, u % 2, grp, own], qt_lo[:, u % 2, grp, own]),
                                       (gk[:, grp, 0, u // DUOS, cols], gk[:, grp, 1, u // DUOS, cols]))])
                    mm.then_inc(g_scores, 1)

            def turn_probs(t, side, before):
                pe.wait_ge(g_probs, t + 1)
                for k, (c0, ncs) in enumerate(T_BANKS):
                    if before:
                        pe.wait_ge(g_pt_lo, 3 * t - 2 + k)
                    for c in range(c0, c0 + ncs):
                        mm = pe.transpose(banks[0:rows_of(c), 3 + k, (c - c0) * P:(c - c0 + 1) * P],
                                          g_pr[:, side, c * P:c * P + rows_of(c)], ident[:, :])
                    mm.then_inc(g_pt_raw, 1)

            def turn_x(m):
                pe.wait_ge(g_xn, d0 + m + 3)
                if duo(m, 0):
                    pe.wait_ge(g_shifted, 6 * (d0 + m) + 5)
                for side in range(2):
                    for ct in range(CT):
                        mm = pe.transpose(banks[:, side, ct * P:(ct + 1) * P], xn[:, side, ct * P:(ct + 1) * P], ident[:, :])
                    mm.then_inc(g_xt_raw, 1)

            def step(m, u):
                d = d0 + m
                if duo(m, 0):
                    pe.wait_ge(g_qt_lo, 2 * d + 2)
                    if only(m, 0):
                        pe.wait_ge(k_built_dve, 2 * (rnd + 1))
                        pe.wait_ge(k_built_act, 2 * (rnd + 1))
                    if duo(m, 1):
                        pe.wait_ge(g_xt_lo, 2 * d + 4)
                    scores(m, u, 0)
                if only(m, 0):
                    spread_v(range(6, 9))
                if duo(m, -1):
                    turn_probs(2 * d - 1, 1, True)
                if duo(m, 1):
                    pe.wait_ge(g_xt_lo, 2 * d + 4)
                    if only(m, -1):
                        pe.wait_ge(wq_lo, CT * (rnd + 1))
                    for g in range(KV_HEADS):
                        if g % 2 == 0 and duo(m, -2):
                            pe.wait_ge(x_updated, a0 + 2 * m - 3 + g // 2)
                        mm = product(pe, banks[:, 6 + g // 2, g % 2 * 2 * P:(g % 2 + 1) * 2 * P],
                                     [((gq_hi[:, ct, g * P:(g + 1) * P], gq_lo[:, ct, g * P:(g + 1) * P]),
                                       (gxt_hi[:, ct, :], gxt_lo[:, ct, :])) for ct in range(CT)])
                        if g % 2:
                            mm.then_inc(g_q, 1)
                        if only(m, -1) and g == 1:
                            turn_x(m)
                        if only(m, -1) and g % 2:
                            spread_v(range(0, 3) if g == 1 else range(3, 5))
                if only(m, 0):
                    spread_v(range(9, BATCH * V_LOADS))
                if duo(m, 0):
                    scores(m, u, 1)
                if duo(m, -1):
                    pe.wait_ge(g_pt_lo, 6 * d)
                    for g in range(KV_HEADS):
                        if g % 2 == 0:
                            if duo(m, 1):
                                pe.wait_ge(g_qt_lo, 2 * d + 3 + g // 2)
                            elif duo(m, 0):
                                pe.wait_ge(x_updated, a0 + 2 * m - 3 + g // 2)
                        mm = product(pe, banks[:, o_bank(m) + g // 2, g % 2 * 2 * P:(g % 2 + 1) * 2 * P],
                                     [((gv[0:rows_of(c), (u - 1) // DUOS, FIRST_SLOT[g] + n, 0, :],
                                         gv[0:rows_of(c), (u - 1) // DUOS, FIRST_SLOT[g] + n, 1, :]),
                                       (gpt_hi[0:rows_of(c), c, :], gpt_lo[0:rows_of(c), c, :]))
                                      for n, c in enumerate(GROUP_CHUNKS[g])])
                        if g % 2:
                            mm.then_inc(g_o, 1)
                if only(m, 0):
                    pe.wait_ge(v_built, BATCH * V_LOADS * (rnd + 1))
                if duo(m, 0):
                    turn_probs(2 * d, 0, duo(m, -1))
                if duo(m, 2) and not only(m, -1):
                    turn_x(m)
                if duo(m, -1):
                    if only(m, 1):
                        pe.wait_ge(wo_lo, rnd + 1)
                    for side in range(2):
                        own = slice(side * P, (side + 1) * P)
                        if not duo(m, 0):
                            pe.wait_ge(x_updated, a0 + 2 * m - 3 + side)
                        for half_of in range(2):
                            pe.wait_ge(g_ot_lo, 2 * d - 1 + half_of)
                            mm = product(pe, banks[:, 6 + side, :], [((ot_hi[:, ct, own], ot_lo[:, ct, own]), (go_hi[:, ct, :], go_lo[:, ct, :]))
                                                                     for ct in (2 * half_of, 2 * half_of + 1)],
                                         first=half_of == 0, last=half_of == 1)
                        mm.then_inc(g_out, 1)

            def start():
                step(-2, -2)

            def rest():
                spread_k()
                step(-1, -1)
                spread_v(range(5, 6))
                sweep(pe, 0, ALL_DUOS, DUO_LOOPS, step)

            return start, rest

        def of_round(w, rnd):
            return w[bass.ds(rnd, 1)].rearrange("r (t p) n -> p (r t) n", p=P)

        def first_weights(act, rnd):
            for half_of, done in ((0, w_first), (1, w_in[0])):
                cols = slice(half_of * 2 * P, (half_of + 1) * 2 * P)
                act.dma_start(wst[0][:, :, cols], of_round(d_wk, rnd)[:, :, cols]).then_inc(done, 16)

        def dense_project_act(act, rnd):
            parts = [of_round(w, rnd)[:, :, q * C:(q + 1) * C] for w in (d_wk, d_wv) for q in range(2)]
            parts += [of_round(d_wq_t, rnd), of_round(d_wo, rnd)]
            act.dma_start(wst[1][:, :, :], parts[1]).then_inc(w_in[1], 16)
            for dst, src in ((tok_sb, token_c), (idx_i, d_idx[bass.ds(rnd, 1)].rearrange("r p n -> p (r n)")),
                             (m_sb[:, 0, :], mask_a), (m_sb[:, 1, :], mask_b),
                             (bo_sb, d_bo[bass.ds(rnd, 1)].rearrange("r p n -> p (r n)"))):
                act.dma_start(dst[:, :], src).then_inc(aux_in, 16)
            for n in range(4):
                for t in range(4 * n, 4 * n + 4):
                    act.wait_ge(proj_done, 16 * rnd + t + 1)
                    act.activation((k_t if t < PAIRS else v_t)[:, t % PAIRS, :], banks[:, t % 8, 0:BATCH * TOK],
                                   ACT.Copy).then_inc(proj_read, 1)
                act.dma_start(wst[n % 2][:, :, :], parts[n + 2]).then_inc(w_in[n % 2], 16)

        def key_table_act(act, visit, numbers):
            for n in numbers:
                ct, h0, nh = GROUPS[n]
                act.wait_ge(kt_raw, visit * len(GROUPS) + n + 1)
                act.activation(kt_hi[:, ct, h0 * TOK:(h0 + nh) * TOK], banks[:, KT_BANKS[n % 4], 0:nh * TOK],
                               ACT.Copy).then_inc(kt_hi_made, 1)

        def value_table_act(act, visit, c):
            r = rows_of(c)
            act.wait_ge(vt_raw, visit * CHUNKS + c + 1)
            act.activation(vt_hi[0:r, c, :], banks[0:r, VT_BANKS[c % 3], :], ACT.Copy).then_inc(vt_hi_made, 1)

        def dense_act(act, rnd, b, start_group):
            visit = rnd * BATCH + b
            g0 = visit * TILES

            def xt_part(i, u):
                act.wait_ge(d_xt_raw, g0 + i + 1)
                if there(i, -2):
                    act.wait_ge(d_scores, 3 * (g0 + i) - 3)
                act.activation(xt_hi[:, u % 2, :, :].rearrange("p t n -> p (t n)"), banks[:, 6, :],
                               ACT.Copy).then_inc(d_xt_hi, 1)

            def step(i, u):
                g = g0 + i
                if only(i, 1) and b == BATCH - 1:
                    for dst, src in ((kv_weights(0), of_round(g_wk, rnd)), (kv_weights(1), of_round(g_wv, rnd)),
                                     (wst[0][:, 4:8, :], of_round(g_wo, rnd)), (wst[1][:, 0:4, :], of_round(g_wq, rnd)),
                                     (norm_sb[:, :], g_norm[bass.ds(rnd, 1)].rearrange("r p n -> p (r n)"))):
                        act.dma_start(dst, src).then_inc(gw_in, 16)
                if there(i, -2):
                    if there(i, -3):
                        act.wait_ge(d_out, g - 2)
                    for k, (c0, ncs) in enumerate(T_BANKS):
                        act.wait_ge(d_pt_raw, 3 * g - 5 + k)
                        copy_probs(act, k, 3 + k, pt_hi[:, :, :]).then_inc(d_pt_hi, 1)
                if only(i, TILES) and b < BATCH - 1:
                    key_table_act(act, visit + 1, range(HALF))
                if only(i, TILES) and b == BATCH - 1:
                    start_group()
                if only(i, TILES + 1) and b < BATCH - 1:
                    key_table_act(act, visit + 1, range(HALF, len(GROUPS)))
                if only(i, 1):
                    xt_part(2, 2)
                if there(i, 1, 3):
                    xt_part(i + 1, u + 1)
                if only(i, 0):
                    value_table_act(act, visit, LATE)
                if there(i, 0):
                    act.wait_ge(d_shifted, g + 1)
                    act.activation(probs[:, u % 2, :], probs[:, u % 2, :], ACT.Exp, scale=DENSE_SCALE).then_inc(d_exp, 1)
                if only(i, 0):
                    for c in range(LATE + 1, CHUNKS):
                        value_table_act(act, visit, c)

            if b == 0:
                key_table_act(act, visit, range(len(GROUPS)))
            for c in range(LATE):
                if c in X_AFTER:
                    xt_part(X_AFTER.index(c), X_AFTER.index(c))
                value_table_act(act, visit, c)
            sweep(act, 0, TILES + 1, [TILE_LOOP], step)

        def copy_probs(act, k, bank, dst):
            c0, ncs = T_BANKS[k]
            full = ncs if rows_of(c0 + ncs - 1) == P else ncs - 1
            ins = act.activation(dst[:, c0:c0 + full, :], banks[:, bank, 0:full * P].rearrange("p (c n) -> p c n", n=P), ACT.Copy)
            if full < ncs:
                c, r = c0 + full, rows_of(c0 + full)
                ins = act.activation(dst[0:r, c, :], banks[0:r, bank, full * P:ncs * P], ACT.Copy)
            return ins

        def rest_of_probs(dve, k, bank, hi, lo):
            c0, ncs = T_BANKS[k]
            full = ncs if rows_of(c0 + ncs - 1) == P else ncs - 1
            at = slice(c0, c0 + full)
            ins = dve.tensor_tensor(lo[:, at, :], banks[:, bank, 0:full * P].rearrange("p (c n) -> p c n", n=P),
                                    hi[:, at, :].bitcast(F32), ALU.subtract)
            if full < ncs:
                c, r = c0 + full, rows_of(c0 + full)
                ins = dve.tensor_tensor(lo[0:r, c, :], banks[0:r, bank, full * P:ncs * P],
                                        hi[0:r, c, :].bitcast(F32), ALU.subtract)
            return ins

        def duo_columns(ap, side):
            return ap[:, :, side * P:(side + 1) * P]

        def ring(m, u, k):
            return slot((2 * m + k) % TILES if isinstance(m, int) else 2 * m + (k - TILES * (u // DUOS)))

        def group_act(act, rnd, x0):
            d0 = rnd * ALL_DUOS

            def probs_part(t, side):
                for k in range(len(T_BANKS)):
                    act.wait_ge(g_pt_raw, 3 * t + k + 1)
                    copy_probs(act, k, 3 + k, duo_columns(gpt_hi[:, :, :], side)).then_inc(g_pt_hi, 1)

            def xt_part(m):
                for side in range(2):
                    act.wait_ge(g_xt_raw, 2 * (d0 + m) + 5 + side)
                    act.activation(duo_columns(gxt_hi[:, :, :], side), banks[:, side, :].rearrange("p (t n) -> p t n", t=CT),
                                   ACT.Copy).then_inc(g_xt_hi, 1)

            def exp(t, side):
                act.wait_ge(g_shifted, 3 * t + 3)
                act.activation(g_pr[:, side, :], g_pr[:, side, :], ACT.Exp, scale=GROUP_SCALE).then_inc(g_exp, 1)

            def step(m, u):
                d = d0 + m
                if only(m, DUO_LOOPS[0][1]):
                    act.wait_ge(wo_lo, rnd + 1)
                    act.sem_inc(passed, 1)
                    first_weights(act, rnd * -1 + (ROUNDS - 1))
                if duo(m, -1):
                    probs_part(2 * d - 1, 1)
                if duo(m, 0):
                    exp(2 * d, 0)
                if duo(m, 1):
                    for half_of in range(2):
                        act.wait_ge(g_q, 2 * d + 3 + half_of)
                        act.activation(qt_hi[:, (u + 1) % 2, 2 * half_of:2 * half_of + 2, :],
                                       banks[:, 6 + half_of, :].rearrange("p (g n) -> p g n", g=2), ACT.Copy).then_inc(g_qt_hi, 1)
                for half_of in range(2):
                    if duo(m, -1):
                        act.wait_ge(g_o, 2 * d - 1 + half_of)
                        act.activation(ot_hi[:, 2 * half_of:2 * half_of + 2, :],
                                       banks[:, o_bank(m) + half_of, :].rearrange("p (g n) -> p g n", g=2), ACT.Copy).then_inc(g_ot_hi, 1)
                    if half_of == 0 and duo(m, 0):
                        exp(2 * d + 1, 1)
                if only(m, 0):
                    xt_part(m)
                if duo(m, 0):
                    probs_part(2 * d, 0)
                if duo(m, 3):
                    act.wait_ge(x_there, x0 + 2 * m + 8)
                    if duo(m, 2):
                        act.wait_ge(g_rms, d + 3)
                    act.sem_inc(passed, 1)
                    for side in range(2):
                        act.activation(squares[:, side, :], ring(m, u, 6 + side), ACT.Square,
                                       accum_out=ssq[:, side:side + 1]).then_inc(g_sq, 1)
                if only(m, -3):
                    act.wait_ge(gw_in, 80 * rnd + 80)
                    for ct in range(CT):
                        act.activation(gq_hi[:, ct, :], wst[1][:, ct, :], ACT.Copy, scale=norm_sb[:, ct:ct + 1]).then_inc(wq_hi, 1)
                if duo(m, 2) and not only(m, 0):
                    xt_part(m)
                if duo(m, 3):
                    act.wait_ge(g_rms, d + 4)
                    act.sem_inc(passed, 1)
                    for side in range(2):
                        ins = act.activation(xn[:, side, :], ring(m, u, 6 + side), ACT.Copy, scale=rms[:, side:side + 1])
                    ins.then_inc(g_xn, 1)

            def start():
                step(-3, -3)

            def rest():
                act.wait_ge(g_proj, 2 * rnd + 1)
                act.activation(k1[:, 0, :], banks[:, 2, 0:BATCH * TOK], ACT.Copy).then_inc(kv_hi, 1)
                act.wait_ge(g_proj, 2 * rnd + 2)
                act.activation(v1[0:TOK, :, 0, :], both_v, ACT.Copy).then_inc(kv_hi, 1)
                step(-2, -2)
                for g in range(2, KV_HEADS):
                    act.wait_ge(k_spread, KV_HEADS * rnd + g + 1)
                    for h in range(4):
                        ins = act.activation(gk[:, g, :, :, h * TOK:(h + 1) * TOK].rearrange("p a b k -> p (a b) k"),
                                             banks[:, K_BANKS[g], 0:2 * BATCH * TOK].rearrange("p (b k) -> p b k", k=TOK),
                                             ACT.Copy, scale=quarter[:, h:h + 1])
                    ins.then_inc(k_built_act, 1)
                act.activation(go_hi[:, :, :], wst[0][:, 4:8, :], ACT.Copy).then_inc(wo_hi, 1)
                sweep(act, -1, ALL_DUOS, DUO_LOOPS, step)

            return start, rest

        BIAS_LINKS = 20

        def bias_dve(dve, rnd):
            links = 0

            def linked(ins):
                nonlocal links
                links += 1
                ins.then_inc(bias_link, 1)
                dve.wait_ge(bias_link, BIAS_LINKS * rnd + links)

            dve.wait_ge(aux_in, 80 * rnd + 80)
            linked(dve.tensor_copy(idx_f[:, 0:4], idx_i[:, :]))
            linked(dve.tensor_scalar(idx_f[:, 4:8], idx_f[:, 0:4], float(TOK), None, ALU.add))
            for n in range(8):
                linked(dve.tensor_scalar(hot[:, n, :], tok_sb[:, :], idx_f[:, n:n + 1], None, ALU.is_equal))
            for n, m in ((0, 1), (0, 4), (0, 5), (2, 3), (2, 6), (2, 7)):
                linked(dve.tensor_tensor(hot[:, n, :], hot[:, n, :], hot[:, m, :], ALU.max))
            linked(dve.tensor_tensor(hot[:, 0, :], hot[:, 0, :], hot[:, 2, :], ALU.is_gt))
            linked(dve.tensor_scalar(m_sb[:, :, :], m_sb[:, :, :], -1.0, 1.0, ALU.mult, ALU.add))

            def outer(dst, s, n):
                mask = m_sb[:, s, :].unsqueeze(2).broadcast_to([P, TILES, TOK])
                token = hot[:, n, :].unsqueeze(1).broadcast_to([P, TILES, TOK])
                return dve.tensor_tensor(dst[:, :, :], mask, token, ALU.mult)

            outer(bias8, 0, 0)
            linked(outer(bias_b, 1, 2))
            linked(dve.tensor_tensor(bias8[:, :, :], bias8[:, :, :], bias_b[:, :, :], ALU.add))
            assert links == BIAS_LINKS
            dve.tensor_scalar(bias8[:, :, :], bias8[:, :, :], -SUPPRESS / DENSE_SCALE, None, ALU.mult)

        def block_diagonal_k(dve, rnd, b):
            dve.tensor_tensor(k_bd[:, :, :].rearrange("p q (h k) -> p q h k", k=TOK),
                              k_t[:, :, b * TOK:(b + 1) * TOK].unsqueeze(2).broadcast_to([P, PAIRS, 2, TOK]),
                              half[:, :].unsqueeze(1).unsqueeze(3).broadcast_to([P, PAIRS, 2, TOK]),
                              ALU.mult).then_inc(kbd_ready, 1)

        def block_diagonal_v(dve, rnd, b):
            dve.wait_ge(zero_done, rnd * BATCH + b + 1)
            for p in range(PAIRS):
                at = WINDOW_AT[p] + 2 * TOK * p - window_start(p)
                ins = dve.tensor_tensor(v_bd[:, at:at + 2 * TOK].rearrange("p (h k) -> p h k", k=TOK),
                                        v_t[:, p, b * TOK:(b + 1) * TOK].unsqueeze(1).broadcast_to([P, 2, TOK]),
                                        half[:, :].unsqueeze(2).broadcast_to([P, 2, TOK]), ALU.mult)
            ins.then_inc(vbd_ready, 1)

        def key_table_dve(dve, visit, numbers):
            for n in numbers:
                ct, h0, nh = GROUPS[n]
                cols = slice(h0 * TOK, (h0 + nh) * TOK)
                dve.wait_ge(kt_hi_made, visit * len(GROUPS) + n + 1)
                dve.tensor_tensor(kt_lo[:, ct, cols], banks[:, KT_BANKS[n % 4], 0:nh * TOK], kt_hi[:, ct, cols].bitcast(F32),
                                  ALU.subtract).then_inc(kt_lo_made, 1)

        def slot(i):
            return x_ring[:, i, :] if isinstance(i, int) else x_ring[:, bass.ds(i, 1), :].rearrange("p a n -> p (a n)")

        def heads3(ap, nh):
            return ap.rearrange("p (h k) -> p h k", h=nh)

        def value_table_dve(dve, visit, c):
            r = rows_of(c)
            dve.wait_ge(vt_hi_made, visit * CHUNKS + c + 1)
            dve.tensor_tensor(vt_lo[0:r, c, :], banks[0:r, VT_BANKS[c % 3], :], vt_hi[0:r, c, :].bitcast(F32),
                              ALU.subtract).then_inc(vt_lo_made, 1)

        def dense_dve(dve, rnd, b, start_group):
            visit = rnd * BATCH + b
            g0, a0 = visit * TILES, (rnd * 2 * BATCH + b) * TILES

            def xt_rest(i, u):
                dve.wait_ge(d_xt_hi, g0 + i + 1)
                dve.tensor_tensor(xt_lo[:, u % 2, :, :].rearrange("p t n -> p (t n)"), banks[:, 6, :],
                                  xt_hi[:, u % 2, :, :].rearrange("p t n -> p (t n)").bitcast(F32), ALU.subtract).then_inc(d_xt_lo, 1)

            def step(i, u):
                g = g0 + i
                pr = probs[:, u % 2, :]
                if there(i, -3):
                    dve.wait_ge(d_out, g - 2)
                    dve.wait_ge(d_bo_added, g - 2)
                    dve.tensor_tensor(slot(i - 3), banks[:, 7, :], slot(i - 3), ALU.add).then_inc(x_updated, 1)
                if there(i, -2):
                    for k in range(3):
                        dve.wait_ge(d_pt_hi, 3 * g - 5 + k)
                        rest_of_probs(dve, k, 3 + k, pt_hi[:, :, :], pt_lo[:, :, :]).then_inc(d_pt_lo, 1)
                if only(i, TILES) and b < BATCH - 1:
                    key_table_dve(dve, visit + 1, range(HALF))
                if only(i, TILES + 1) and b < BATCH - 1:
                    key_table_dve(dve, visit + 1, range(HALF, len(GROUPS)))
                    block_diagonal_v(dve, rnd, b + 1)
                if only(i, TILES + 1) and b == BATCH - 1:
                    start_group()
                if only(i, 1):
                    xt_rest(2, 2)
                if there(i, 0):
                    bias = bias8[:, i, :] if isinstance(i, int) else bias8[:, bass.ds(i, 1), :].rearrange("p a n -> p (a n)")
                    for k, (h0, nh) in enumerate(S_BANKS):
                        dve.wait_ge(d_scores, 3 * g + k + 1)
                        dve.tensor_tensor(heads3(pr[:, h0 * TOK:(h0 + nh) * TOK], nh), heads3(banks[:, k, 0:nh * TOK], nh),
                                          bias.unsqueeze(1).broadcast_to([P, nh, TOK]), ALU.add).then_inc(d_biased, 1)
                if there(i, 1, 3):
                    xt_rest(i + 1, u + 1)
                if there(i, 0):
                    wide = heads3(pr, HEADS)
                    dve.wait_ge(d_biased, 3 * g + 3)
                    dve.tensor_reduce(row_max, wide, X, ALU.max).then_inc(d_max, 1)
                    dve.wait_ge(d_max, g + 1)
                    dve.tensor_tensor(wide, wide, row_max.unsqueeze(2).broadcast_to([P, HEADS, TOK]),
                                      ALU.subtract).then_inc(d_shifted, 1)
                    if only(i, 0):
                        value_table_dve(dve, visit, LATE)
                    dve.wait_ge(d_exp, g + 1)
                    dve.tensor_reduce(row_sum, wide, X, ALU.add).then_inc(d_sum, 1)
                    dve.wait_ge(d_sum, g + 1)
                    dve.reciprocal(row_rcp, row_sum).then_inc(d_rcp, 1)
                    dve.wait_ge(d_rcp, g + 1)
                    dve.tensor_tensor(wide, wide, row_rcp.unsqueeze(2).broadcast_to([P, HEADS, TOK]),
                                      ALU.mult).then_inc(d_probs, 1)
                    if only(i, 0):
                        for c in range(LATE + 1, CHUNKS):
                            value_table_dve(dve, visit, c)
                if only(i, TILES - 2) and b < BATCH - 1:
                    block_diagonal_k(dve, rnd, b + 1)

            if b == 0:
                dve.wait_ge(proj_read, 16 * rnd + PAIRS)
                block_diagonal_k(dve, rnd, b)
                dve.wait_ge(proj_read, 16 * rnd + 2 * PAIRS)
                block_diagonal_v(dve, rnd, b)
                key_table_dve(dve, visit, range(len(GROUPS)))
            for c in range(LATE):
                if c in X_AFTER:
                    xt_rest(X_AFTER.index(c), X_AFTER.index(c))
                value_table_dve(dve, visit, c)
            sweep(dve, 0, TILES + 2, [TILE_LOOP], step)

        def group_dve(dve, rnd):
            d0 = rnd * ALL_DUOS

            def build_v(numbers):
                for at in numbers:
                    b, n = at // V_LOADS, at % V_LOADS
                    bank = 3 + at % V_BANKS
                    dve.wait_ge(v_spread, BATCH * V_LOADS * rnd + at + 1)
                    for c in (2 * n, 2 * n + 1):
                        r = rows_of(c)
                        rows = banks[0:r, bank, c % 2 * 2 * P:(c % 2 + 1) * 2 * P].rearrange("p (a n) -> p a n", a=2)
                        for g in range(KV_HEADS):
                            if c not in GROUP_CHUNKS[g]:
                                continue
                            s0 = FIRST_SLOT[g] + c - GROUP_CHUNKS[g][0]
                            ins = dve.tensor_tensor(gv[0:r, b, s0, :, :].rearrange("p a (r n) -> p a r n", r=4),
                                                    rows[:, :, g * GROUP_D:(g + 1) * GROUP_D].unsqueeze(2).broadcast_to([r, 2, 4, GROUP_D]),
                                                    member[0:r, s0, :].unsqueeze(1).unsqueeze(3).broadcast_to([r, 2, 4, GROUP_D]),
                                                    ALU.mult)
                    ins.then_inc(v_built, 1)

            def shift(t, side):
                for k, (h0, nh) in enumerate(S_BANKS):
                    scores = heads3(banks[:, k, 0:nh * TOK], nh)
                    top = g_row_max[:, h0:h0 + nh]
                    dve.wait_ge(g_scores, 3 * t + k + 1)
                    dve.tensor_reduce(top, scores, X, ALU.max).then_inc(g_max, 1)
                    dve.wait_ge(g_max, 3 * t + k + 1)
                    dve.tensor_tensor(heads3(g_pr[:, side, h0 * TOK:(h0 + nh) * TOK], nh), scores,
                                      top.unsqueeze(2).broadcast_to([P, nh, TOK]), ALU.subtract).then_inc(g_shifted, 1)

            def denominators(t, side):
                dve.wait_ge(g_exp, t + 1)
                dve.tensor_reduce(g_sum[side], heads3(g_pr[:, side, :], HEADS), X, ALU.add).then_inc(g_sum_done, 1)
                dve.wait_ge(g_sum_done, t + 1)
                dve.reciprocal(g_rcp_of[side], g_sum[side]).then_inc(g_rcp, 1)

            def probs_rest(t, side):
                for k in range(len(T_BANKS)):
                    dve.wait_ge(g_pt_hi, 3 * t + k + 1)
                    rest_of_probs(dve, k, 3 + k, duo_columns(gpt_hi[:, :, :], side), duo_columns(gpt_lo[:, :, :], side)).then_inc(g_pt_lo, 1)

            def two_groups(ap, n):
                return ap.rearrange("p (g n) -> p g n", g=n)

            def q_rest(d, u, half_of):
                dve.wait_ge(g_qt_hi, 2 * d + 3 + half_of)
                own = slice(2 * half_of, 2 * half_of + 2)
                dve.tensor_tensor(qt_lo[:, (u + 1) % 2, own, :], two_groups(banks[:, 6 + half_of, :], 2),
                                  qt_hi[:, (u + 1) % 2, own, :].bitcast(F32), ALU.subtract).then_inc(g_qt_lo, 1)

            def xt_rest(m):
                for side in range(2):
                    dve.wait_ge(g_xt_hi, 2 * (d0 + m) + 5 + side)
                    dve.tensor_tensor(duo_columns(gxt_lo[:, :, :], side), two_groups(banks[:, side, :], CT),
                                      duo_columns(gxt_hi[:, :, :], side).bitcast(F32), ALU.subtract).then_inc(g_xt_lo, 1)

            def step(m, u):
                d = d0 + m
                if duo(m, 0):
                    shift(2 * d, 0)
                if duo(m, -1):
                    probs_rest(2 * d - 1, 1)
                if only(m, 0):
                    build_v(range(6, 8))
                if duo(m, 1):
                    q_rest(d, u, 0)
                if only(m, -1):
                    build_v(range(0, 3))
                if duo(m, 0):
                    denominators(2 * d, 0)
                if only(m, 0):
                    build_v(range(8, 9))
                if duo(m, 1):
                    q_rest(d, u, 1)
                if only(m, 0):
                    build_v(range(9, BATCH * V_LOADS))
                if duo(m, 0):
                    shift(2 * d + 1, 1)
                if duo(m, -1):
                    for half_of in range(2):
                        own = slice(2 * half_of, 2 * half_of + 2)
                        dve.wait_ge(g_ot_hi, 2 * d - 1 + half_of)
                        dve.tensor_tensor(ot_lo[:, own, :], two_groups(banks[:, o_bank(m) + half_of, :], 2),
                                          ot_hi[:, own, :].bitcast(F32), ALU.subtract).then_inc(g_ot_lo, 1)
                if only(m, 0):
                    xt_rest(m)
                if duo(m, 0):
                    denominators(2 * d + 1, 1)
                    probs_rest(2 * d, 0)
                if duo(m, 2) and not only(m, 0):
                    xt_rest(m)
                if duo(m, -1):
                    for side in range(2):
                        dve.wait_ge(g_out, 2 * d - 1 + side)
                        own = ring(m, u, side - 2)
                        dve.tensor_tensor(own, banks[:, 6 + side, :], own, ALU.add).then_inc(x_updated, 1)

            def start():
                for ct in range(CT):
                    dve.wait_ge(wq_hi, CT * rnd + ct + 1)
                    dve.scalar_tensor_tensor(gq_lo[:, ct, :], wst[1][:, ct, :], norm_sb[:, ct:ct + 1], gq_hi[:, ct, :].bitcast(F32),
                                             ALU.mult, ALU.subtract).then_inc(wq_lo, 1)
                dve.wait_ge(kv_hi, 2 * rnd + 1)
                dve.tensor_tensor(k1[:, 1, :], banks[:, 2, 0:BATCH * TOK], k1[:, 0, :].bitcast(F32), ALU.subtract).then_inc(kv_lo, 1)
                dve.wait_ge(kv_hi, 2 * rnd + 2)
                dve.tensor_tensor(v1[0:TOK, :, 1, :], both_v, v1[0:TOK, :, 0, :].bitcast(F32), ALU.subtract).then_inc(kv_lo, 1)
                step(-2, -2)

            def rest():
                for g in range(2):
                    dve.wait_ge(k_spread, KV_HEADS * rnd + g + 1)
                    dve.tensor_tensor(gk[:, g, :, :, :].rearrange("p a b (r k) -> p (a b) r k", k=TOK),
                                      banks[:, K_BANKS[g], 0:2 * BATCH * TOK].rearrange("p (b k) -> p b k", k=TOK).unsqueeze(2)
                                      .broadcast_to([P, 2 * BATCH, 4, TOK]),
                                      quarter[:, :].unsqueeze(1).unsqueeze(3).broadcast_to([P, 2 * BATCH, 4, TOK]),
                                      ALU.mult).then_inc(k_built_dve, 1)
                step(-1, -1)
                build_v(range(3, 6))
                sweep(dve, 0, ALL_DUOS, DUO_LOOPS, step)

            return start, rest


        def group_pool(pool, rnd):
            d0 = rnd * ALL_DUOS

            def normalise(t, side):
                pool.wait_ge(g_rcp, t + 1)
                wide = heads3(g_pr[:, side, :], HEADS)
                pool.tensor_tensor(wide, wide, g_rcp_of[side].unsqueeze(2).broadcast_to([P, HEADS, TOK]),
                                   ALU.mult).then_inc(g_probs, 1)

            def step(m, u):
                d = d0 + m
                if duo(m, 0):
                    normalise(2 * d, 0)
                    normalise(2 * d + 1, 1)
                if duo(m, 3):
                    pool.wait_ge(g_sq, 2 * d + 8)
                    if duo(m, 2):
                        pool.wait_ge(g_xn, d + 3)
                    pool.sem_inc(passed, 1)
                    pool.tensor_scalar(mean_sq, ssq, 1.0 / C, EPS, ALU.mult, ALU.add).then_inc(g_var, 1)
                    pool.wait_ge(g_var, d + 4)
                    pool.tensor_tensor(rms, mean_sq, exponent, ALU.pow).then_inc(g_rms, 1)

            for m in range(-3, 0):
                step(m, m)
            pool.wait_ge(wo_hi, rnd + 1)
            pool.sem_inc(passed, 1)
            pool.tensor_tensor(go_lo[:, :, :], wst[0][:, 4:8, :], go_hi[:, :, :].bitcast(F32), ALU.subtract).then_inc(wo_lo, 1)
            sweep(pool, 0, ALL_DUOS - 1, DUO_LOOPS, step)

        block = ctx.enter_context(nc.Block())

        @block.tensor
        def _(pe):
            pe.wait_ge(const_in, 16 * 5)
            with pe.Fori(0, ROUNDS) as rnd:
                for n in range(4):
                    for m in range(4):
                        t = 4 * n + m
                        if n == 0:
                            if m == 0:
                                pe.wait_ge(w_first, 16 * rnd + 16)
                            if m == 2:
                                pe.wait_ge(w_in[0], 48 * rnd + 16)
                        elif m == 0:
                            pe.wait_ge(w_in[n % 2], 48 * rnd + 16 * (n // 2 + 1))
                        if t >= 8:
                            pe.wait_ge(proj_read, 16 * rnd + t - 7)
                        for kt in range(XT):
                            mm = pe.matmul(banks[:, t % 8, 0:BATCH * TOK], wst[n % 2][:, kt, m * P:(m + 1) * P],
                                           ctx_sb[:, kt, :], start=kt == 0, stop=kt == XT - 1)
                        mm.then_inc(proj_done, 1)
                start_group, rest_of_group = group_pe(pe, rnd, (rnd * 2 * BATCH + BATCH) * TILES)
                for b in range(BATCH):
                    dense_pe(pe, rnd, b, start_group)
                rest_of_group()
                round_end(pe, rnd)

        @block.scalar
        def _(act):
            act.wait_ge(consts_raw, 16 * 2)
            act.activation(select[:, :], select_raw[:, :], ACT.Copy)
            act.activation(spread[:, :], spread_raw[:, :], ACT.Copy)
            assert ROUNDS == 2
            first_weights(act, 0)
            with act.Fori(0, ROUNDS) as rnd:
                dense_project_act(act, rnd)
                start_group, rest_of_group = group_act(act, rnd, (rnd * 2 * BATCH + BATCH) * TILES)
                for b in range(BATCH):
                    dense_act(act, rnd, b, start_group)
                rest_of_group()
                round_end(act, rnd)
            act.wait_ge(w_first, 16 * (ROUNDS + 1))
            act.wait_ge(w_in[0], 48 * ROUNDS + 16)

        @block.vector
        def _(dve):
            dve.wait_ge(const_in, 16 * 5)
            with dve.Fori(0, ROUNDS) as rnd:
                bias_dve(dve, rnd)
                start_group, rest_of_group = group_dve(dve, rnd)
                for b in range(BATCH):
                    dense_dve(dve, rnd, b, start_group)
                rest_of_group()
                round_end(dve, rnd)

        @block.gpsimd
        def _(pool):
            pool.memset(exponent, -0.5).then_inc(exponent_set, 1)
            pool.wait_ge(exponent_set, 1)
            with pool.Fori(0, ROUNDS) as rnd:
                for b in range(BATCH):
                    stage, g = rnd * 2 * BATCH + b, (rnd * BATCH + b) * TILES
                    if b == 0:
                        pool.memset(v_bd[:, :], 0.0).then_inc(zero_done, 1)
                        pool.wait_ge(aux_in, 80 * rnd + 80)
                    for i in range(TILES):
                        if i == 2 and b > 0:
                            pool.wait_ge(d_pt_raw, 3 * g)
                            pool.sem_inc(passed, 1)
                            pool.memset(v_bd[:, :], 0.0).then_inc(zero_done, 1)
                        pool.wait_ge(x_in[i], 16 * stage + 16)
                        if i >= 2 or b > 0:
                            pool.wait_ge(d_xt_raw, g + i - 1)
                        pool.sem_inc(passed, 1)
                        pool.tensor_copy(xs[:, i % 2, :], x_ring[:, i, :]).then_inc(xs_ready, 1)
                        pool.tensor_tensor(x_ring[:, i, :], x_ring[:, i, :], bo_sb[:, :], ALU.add).then_inc(d_bo_added, 1)
                group_pool(pool, rnd)
                round_end(pool, rnd)

        @block.sync
        def _(sp):
            sp.dma_start(ctx_sb[:, :, :], ctx_t.rearrange("(t p) n -> p t n", p=P)).then_inc(const_in, 16)
            for dst, src in ((ident[:, :], ident_c), (half[:, :], half_c), (quarter[:, :], quarter_c), (member[:, :, :], member_c)):
                sp.dma_start(dst, src).then_inc(const_in, 16)
            sp.dma_start(select_raw[:, :], select_c).then_inc(consts_raw, 16)
            sp.dma_start(spread_raw[:, :], spread_c).then_inc(consts_raw, 16)
            x_t = x.rearrange("b (t p) n -> b t p n", p=P)
            out_t = out.rearrange("b (t p) n -> b t p n", p=P)
            sp.wait_ge(w_in[0], 48)
            for i in range(TILES):
                sp.dma_start(x_ring[:, i, :], x_t[0, i]).then_inc(x_in[i], 16)

            def announce(i, s):
                sp.wait_ge(x_in[i], 16 * s + 16)
                sp.sem_inc(x_there, 1)

            for i in range(TILES - AHEAD):
                announce(i, 0)

            def stage(s, dst, src, src_ready=None):
                def load(i):
                    sp.wait_ge(x_out[i], 16 * s + 16)
                    sp.dma_start(x_ring[:, i, :], src[i]).then_inc(x_in[i], 16)

                for i in range(TILES):
                    sp.wait_ge(x_updated, TILES * s + i + 1)
                    sp.dma_start(dst[i], x_ring[:, i, :]).then_inc(x_out[i], 16)
                    if src is not None and i >= 1:
                        load(i - 1)
                    if i < AHEAD:
                        announce(i + TILES - AHEAD, s)
                    elif src is not None:
                        announce(i - AHEAD, s + 1)
                if src is not None:
                    load(TILES - 1)

            stage(0, x_mid[0], x_t[1])
            stage(1, x_mid[1], x_mid[0])
            with sp.Fori(1, ROUNDS * 2 - 1) as t:
                stage(2 * t, x_mid[0], x_mid[1])
                stage(2 * t + 1, x_mid[1], x_mid[0])
            stage(ROUNDS * 4 - 2, out_t[0], x_mid[1])
            stage(ROUNDS * 4 - 1, out_t[1], None)
            for i in range(TILES):
                sp.wait_ge(x_out[i], 16 * ROUNDS * 4)


def constants():
    rows = np.arange(P)
    member = np.zeros((P, SLOTS, 4), np.float32)
    for g, chunks in enumerate(GROUP_CHUNKS):
        for n, c in enumerate(chunks):
            member[:, FIRST_SLOT[g] + n] = (c * P + rows[:, None]) // TOK == 4 * g + np.arange(4)
    return {
        "ident_c": np.eye(P, dtype=np.float32),
        "half_c": (rows[:, None] // DENSE_D == np.arange(2)).astype(np.float32),
        "quarter_c": (rows[:, None] // GROUP_D == np.arange(4)).astype(np.float32),
        "member_c": member,
        "select_c": (np.arange(TOK + P)[None, :] % TOK == np.arange(TOK)[:, None]).astype(np.float32),
        "spread_c": np.concatenate([(rows[:, None] == g * GROUP_D + rows[None, :] % GROUP_D).astype(np.float32)
                                    for g in range(KV_HEADS)], axis=1),
        "token_c": np.ascontiguousarray(np.broadcast_to(np.arange(TOK, dtype=np.float32), (P, TOK))),
    }


def kernel(**inputs):
    import concourse.bacc as bacc
    from concourse.bass_utils import run_bass_kernel_spmd as run

    a = {k: np.asarray(v) for k, v in inputs.items()}

    def both(name):
        return np.stack([a[f"L{n}_xattn_{name}"] for n in (0, 2)])

    def both_g(name):
        return np.stack([a[f"L{n}_xattn_{name}"] for n in (1, 3)])

    def on_rows(v):
        return np.broadcast_to(v[:, None, :], (v.shape[0], P, v.shape[1]))

    arrays = {
        "x": a["x"],
        "ctx_t": a["ctx_2048"].reshape(BATCH * TOK, CTX).T,
        "mask_a": a["mask_S_fk1"].reshape(TILES, P).T,
        "mask_b": a["mask_S_fk0"].reshape(TILES, P).T,
        "d_wq_t": both("Wq").transpose(0, 2, 1),
        "d_wk": both("Wk"),
        "d_wv": both("Wv"),
        "d_wo": both("Wo"),
        "d_bo": on_rows(both("bo")),
        "d_idx": on_rows(np.concatenate([both("token_indices_A"), both("token_indices_B")], axis=1)),
        "g_wq": both_g("wq"),
        "g_wk": both_g("wk"),
        "g_wv": both_g("wv"),
        "g_wo": both_g("wo"),
        "g_norm": both_g("norm_w").reshape(ROUNDS, CT, P).transpose(0, 2, 1),
        **constants(),
    }
    arrays = {k: np.ascontiguousarray(v) for k, v in arrays.items()}
    nc = bacc.Bacc("TRN2", target_bir_lowering=False, num_devices=1)
    args = [nc.dram_tensor(k, v.shape, mybir.dt.from_np(v.dtype), kind="ExternalInput").ap() for k, v in arrays.items()]
    out = nc.dram_tensor("out", (BATCH, ROWS, C), F32, kind="ExternalOutput").ap()
    build(nc, *args, out)
    r = run(nc, [arrays], core_ids=[0])
    return r.results[0]["out"]
```
